# Optimizing a Trainium2 kernel written in Bass

```python
import numpy as np
import jax
import jax.numpy as jnp

def _softmax(x, axis=-1):
    return jax.nn.softmax(x, axis=axis)

def _gelu(x):
    return jax.nn.gelu(x, approximate=True)

def _silu(x):
    return jax.nn.silu(x)

def _sigmoid(x):
    return jax.nn.sigmoid(x)

def _layernorm(x, axis=-1, eps=1e-05):
    m = jnp.mean(x, axis=axis, keepdims=True)
    v = jnp.var(x, axis=axis, keepdims=True)
    return (x - m) / jnp.sqrt(v + eps)

def _scatter_add(tgt, idx, src, axis=0):
    return tgt.at[idx].add(src)

def _segment_sum(src, seg, n):
    return jax.ops.segment_sum(src, seg, n)
kernel_name = 'mk_prb_d1_jaxref_r8_842d31'

def setup_inputs(seed: int=0):
    np.random.seed(seed)
    _w = jnp.asarray

    def _L0_attn_setup():
        import jax, jax.numpy as jnp
        import numpy as np
        HIDDEN = 128
        NUM_HEADS = 16
        HEAD_DIM = 64
        NUM_KV_HEADS = 4

        def _xavier(key, out_dim, in_dim):
            limit = jnp.sqrt(6.0 / (in_dim + out_dim)).astype(jnp.float32)
            return jax.random.uniform(key, (out_dim, in_dim), jnp.float32, -limit, limit)
        key = jax.random.key(seed)
        kx, kq, kk, kv, ko = jax.random.split(key, 5)
        return {'hidden_states': jax.random.normal(kx, (2, 256, HIDDEN), jnp.float32), 'Wq': _xavier(kq, NUM_HEADS * HEAD_DIM, HIDDEN), 'Wk': _xavier(kk, NUM_KV_HEADS * HEAD_DIM, HIDDEN), 'Wv': _xavier(kv, NUM_KV_HEADS * HEAD_DIM, HIDDEN), 'Wo': _xavier(ko, HIDDEN, NUM_HEADS * HEAD_DIM)}
    _L0_attn_in = _L0_attn_setup()

    def _L0_ffn_setup():
        import jax, jax.numpy as jnp
        import numpy as np
        D, FF, E, K = (128, 128, 8, 2)
        B, S = (4, 128)

        def _gelu(x):
            return jax.nn.gelu(x, approximate=False)
        key = jax.random.key(seed)
        ks = jax.random.split(key, 12)
        s = 0.02
        return {'x': jax.random.normal(ks[0], (B, S, D), jnp.float32), 'gate_w': jax.random.normal(ks[1], (D, E), jnp.float32) * s, 'gate_b': jnp.zeros((E,), jnp.float32), 'sw1': jax.random.normal(ks[2], (D, FF), jnp.float32) * s, 'sb1': jnp.zeros((FF,), jnp.float32), 'sw2': jax.random.normal(ks[3], (FF, D), jnp.float32) * s, 'sb2': jnp.zeros((D,), jnp.float32), 'w1': jax.random.normal(ks[4], (E, D, FF), jnp.float32) * s, 'b1': jnp.zeros((E, FF), jnp.float32), 'w2': jax.random.normal(ks[5], (E, FF, D), jnp.float32) * s, 'b2': jnp.zeros((E, D), jnp.float32)}
    _L0_ffn_in = _L0_ffn_setup()
    _d = {'L0_attn_hidden_states': _L0_attn_in['hidden_states'], 'L0_attn_Wq': _L0_attn_in['Wq'], 'L0_attn_Wk': _L0_attn_in['Wk'], 'L0_attn_Wv': _L0_attn_in['Wv'], 'L0_attn_Wo': _L0_attn_in['Wo'], 'L0_ffn_gate_w': _L0_ffn_in['gate_w'], 'L0_ffn_gate_b': _L0_ffn_in['gate_b'], 'L0_ffn_sw1': _L0_ffn_in['sw1'], 'L0_ffn_sb1': _L0_ffn_in['sb1'], 'L0_ffn_sw2': _L0_ffn_in['sw2'], 'L0_ffn_sb2': _L0_ffn_in['sb2'], 'L0_ffn_w1': _L0_ffn_in['w1'], 'L0_ffn_b1': _L0_ffn_in['b1'], 'L0_ffn_w2': _L0_ffn_in['w2'], 'L0_ffn_b2': _L0_ffn_in['b2']}
    _x0 = _d['L0_attn_hidden_states']
    _d['L0_attn_hidden_states'] = jax.random.normal(jax.random.fold_in(jax.random.key(seed), 1), (1, 2048, 128), dtype=_x0.dtype)
    del _x0
    return _d

def reference(L0_attn_hidden_states, L0_attn_Wq, L0_attn_Wk, L0_attn_Wv, L0_attn_Wo, L0_ffn_gate_w, L0_ffn_gate_b, L0_ffn_sw1, L0_ffn_sb1, L0_ffn_sw2, L0_ffn_sb2, L0_ffn_w1, L0_ffn_b1, L0_ffn_w2, L0_ffn_b2):

    def _L0_attn_ref(hidden_states, Wq, Wk, Wv, Wo):
        import jax, jax.numpy as jnp
        import numpy as np
        HIDDEN = 128
        NUM_HEADS = 16
        HEAD_DIM = 64
        NUM_KV_HEADS = 4

        def _xavier(key, out_dim, in_dim):
            limit = jnp.sqrt(6.0 / (in_dim + out_dim)).astype(jnp.float32)
            return jax.random.uniform(key, (out_dim, in_dim), jnp.float32, -limit, limit)
        B, S, _ = hidden_states.shape
        q = (hidden_states @ Wq.T).reshape(B, S, NUM_HEADS, HEAD_DIM).transpose(0, 2, 1, 3)
        k = (hidden_states @ Wk.T).reshape(B, S, NUM_KV_HEADS, HEAD_DIM).transpose(0, 2, 1, 3)
        v = (hidden_states @ Wv.T).reshape(B, S, NUM_KV_HEADS, HEAD_DIM).transpose(0, 2, 1, 3)
        n_rep = NUM_HEADS // NUM_KV_HEADS
        if n_rep > 1:
            k = jnp.repeat(k, n_rep, axis=1)
            v = jnp.repeat(v, n_rep, axis=1)
        scale = HEAD_DIM ** (-0.5)
        scores = jnp.einsum('bhqd,bhkd->bhqk', q, k) * scale
        causal = jnp.triu(jnp.full((S, S), -jnp.inf, dtype=scores.dtype), k=1)
        scores = scores + causal[None, None]
        probs = jax.nn.softmax(scores, axis=-1)
        out = jnp.einsum('bhqk,bhkd->bhqd', probs, v)
        out = out.transpose(0, 2, 1, 3).reshape(B, S, NUM_HEADS * HEAD_DIM)
        return out @ Wo.T

    def _L0_ffn_ref(x, gate_w, gate_b, sw1, sb1, sw2, sb2, w1, b1, w2, b2):
        import jax, jax.numpy as jnp
        import numpy as np
        D, FF, E, K = (128, 128, 8, 2)
        B, S = (4, 128)

        def _gelu(x):
            return jax.nn.gelu(x, approximate=False)
        Bb, Ss, Dm = x.shape
        t = x.reshape(-1, Dm)
        T = t.shape[0]
        shared = _gelu(t @ sw1 + sb1) @ sw2 + sb2
        probs = jax.nn.softmax(t @ gate_w + gate_b, axis=-1)
        topk_p, topk_i = jax.lax.top_k(probs, K)
        combine = jnp.zeros((T, E), t.dtype).at[jnp.arange(T)[:, None], topk_i].set(topk_p)
        h = _gelu(jnp.einsum('td,edf->etf', t, w1) + b1[:, None, :])
        y = jnp.einsum('etf,efd->etd', h, w2) + b2[:, None, :]
        routed = jnp.einsum('te,etd->td', combine, y)
        return (routed + shared).reshape(Bb, Ss, Dm)
    x = L0_attn_hidden_states
    xn = _layernorm(x, axis=-1)
    x = x + _L0_attn_ref(xn, L0_attn_Wq, L0_attn_Wk, L0_attn_Wv, L0_attn_Wo) + _L0_ffn_ref(xn, L0_ffn_gate_w, L0_ffn_gate_b, L0_ffn_sw1, L0_ffn_sb1, L0_ffn_sw2, L0_ffn_sb2, L0_ffn_w1, L0_ffn_b1, L0_ffn_w2, L0_ffn_b2)
    return x

_drawn_inputs = setup_inputs


def setup_inputs(seed=0):
    import zlib

    import numpy as np

    out = dict(_drawn_inputs(seed))
    spreads = {'L0_ffn_gate_b': (0.0, 0.51),
     'L0_ffn_sb1': (0.0, 0.755),
     'L0_ffn_sb2': (0.0, 0.1),
     'L0_ffn_b1': (0.0, 0.8),
     'L0_ffn_b2': (0.0, 0.361)}
    factors = {'L0_ffn_gate_w': 2.872, 'L0_ffn_w1': 8.0, 'L0_ffn_w2': 8.0}
    for name, (base, spread) in spreads.items():
        noise = np.random.default_rng([zlib.crc32(name.encode()), seed]).standard_normal(out[name].shape)
        drawn = base * np.exp(spread * noise) if base else spread * noise
        out[name] = jnp.asarray(drawn.astype(out[name].dtype))
    for name, factor in factors.items():
        out[name] = (out[name] * factor).astype(out[name].dtype)
    return out
```

```python
import concourse.bass as bass
from concourse import mybir
from contextlib import ExitStack

P = 128
S = 2048
D = 128
HD = 64
KV = 4
REP = 4
H = KV * REP
E = 8
NE = E + 1
NT = S // P
CH = 4
NC = NT // CH
W = CH * P
EPS = 1e-5
SCALE = HD ** -0.5
NEG = -1e30

NG = NT * KV
NQ = 4
NP = 6
NST = 3
LAG = 2

GROUPS = [(g // KV, g % KV) for g in range(NG)]
UNITS = [(g, i, qt - i) for g, (qt, kv) in enumerate(GROUPS) for i in range(qt + 1)]
FIRST = [next(u for u, x in enumerate(UNITS) if x[0] == g) for g in range(NG)]
COUNT = [qt + 1 for qt, _ in GROUPS]
LAST = [FIRST[g] + COUNT[g] - 1 for g in range(NG)]
NU = len(UNITS)


def max_chunks(g):
    left, at, out = COUNT[g] * P, 0, []
    while left:
        w = min(left, W)
        if left - w == P:
            w -= P
        out.append((at, w))
        at, left = at + w, left - w
    return out


def max_steps(g):
    return [("M", g, h, c) for h in range(REP) for c in range(len(max_chunks(g)))]


def steps_in(g):
    m = max_steps(g + 2) if g + 2 < NG else []
    r = [("R", g + 1, 0, 0)] if g + 1 < NG else []
    q = [("Q", g + 3, 0, 0)] if g + 3 < NG else []
    return m[:2] + r + q + m[2:]


def steps_of(u):
    g, i, _ = UNITS[u]
    s, n = steps_in(g), COUNT[g]
    return s[len(s) * i // n:len(s) * (i + 1) // n]


EARLY = {7: [("C", 0, 0, 0)], 8: [("C", 1, 0, 0)], 10: [("C", 2, 0, 0)], 12: [("C", 3, 0, 0)],
         18: [("Q", 0, 0, 0)], 20: [("Q", 1, 0, 0)], 22: [("Q", 2, 0, 0)],
         24: max_steps(0), 27: [("R", 0, 0, 0)], 28: max_steps(1)}
NF = NC * NE

STREAM = [s for n in range(NF) for s in EARLY.get(n, [])] + [s for u in range(NU) for s in steps_of(u)]
MORDER = {s: n for n, s in enumerate(x for x in STREAM if x[0] == "M")}

ADDS = []
for _g, _i, _j in UNITS:
    ADDS.append((ADDS[-1] if ADDS else 0) + (1 if _i > 0 or COUNT[_g] == 1 else 0))


def added(u):
    g, i, _ = UNITS[u]
    return ADDS[u + 1] if i == 0 and COUNT[g] > 1 else ADDS[u]


def layer(nc, x, wqT, wkT, wvT, woT, gw, gb, b1T, w1, sw1, w2, sw2, b2, sb2, out):
    f32, f32r = mybir.dt.float32, mybir.dt.float32r
    ALU, ACT, AX = mybir.AluOpType, mybir.ActivationFunctionType, mybir.AxisListType

    ctx = ExitStack()
    with ctx:
        def sb(name, shape, dt=f32):
            return ctx.enter_context(nc.sbuf_tensor(name, shape, dt))

        def sem(name):
            return ctx.enter_context(nc.semaphore(name))

        wq_sb = sb("wq_sb", [P, H * HD])
        wk_sb = sb("wk_sb", [P, KV * HD])
        wv_sb = sb("wv_sb", [P, KV * HD])
        wo_sb = sb("wo_sb", [P, H // 2, D])
        gw_sb = sb("gw_sb", [P, E])
        gb_sb = sb("gb_sb", [1, E])
        w1_sb = sb("w1_sb", [P, NE, D])
        w2_sb = sb("w2_sb", [P, NE, D])
        b1_sb = sb("b1_sb", [P, NE])
        b2_sb = sb("b2_sb", [NE, D])
        ident = sb("ident", [P, P])
        negident = sb("negident", [P, P])
        ones = sb("ones", [P, P])
        ones_r = sb("ones_r", [P, HD + 1], f32r)
        causal = sb("causal", [P, W])
        x_sb = sb("x_sb", [P, NT, D])
        xn = sb("xn", [P, NT, D])
        xnT = sb("xnT", [P, S])
        stats = sb("stats", [P, NT, 6])
        mv = sb("mv", [P, NT, 2])
        vare = sb("vare", [P, NT])
        std = sb("std", [P, NT])
        r0 = sb("r0", [P, NT])
        r1 = sb("r1", [P, NT])
        rstd = sb("rstd", [P, NT])
        k_hl = sb("k_hl", [P, KV, S], f32r)
        k_h1 = sb("k_h1", [HD + 1, KV, S], f32r)
        v_sb = sb("v_sb", [P, NT, KV * HD])
        lg = sb("lg", [P, NT, E])
        gmax = sb("gmax", [P, NT])
        gexp = sb("gexp", [P, NT, E])
        gsum = sb("gsum", [P, NT])
        grec = sb("grec", [P, NT])
        gp = sb("gp", [P, NT, 2 * E])
        top = sb("top", [P, NT, E])
        rest = sb("rest", [P, NT, 2 * E])
        comb = sb("comb", [P, NT, NE])
        combT = sb("combT", [NE, S])
        hT = sb("hT", [P, 3, W])
        yacc = sb("yacc", [P, NT, D])
        q_hh = sb("q_hh", [P, NQ, W], f32r)
        q_lm = sb("q_lm", [HD + 1, NQ, W], f32r)
        part = sb("part", [P, 2, REP, 4])
        gmx = sb("gmx", [P, 2, REP])
        diag = sb("diag", [P, 2, W], f32r)
        junk = sb("junk", [P, W])
        pT = sb("pT", [P, NP, W])
        acc = sb("acc", [P, 2, W])
        rec = sb("rec", [P, 2, W // 2])
        on = sb("on", [P, 2, W // 2])

        bank = [ctx.enter_context(nc.psum_tensor(f"bank{n}", [P, W], f32)) for n in range(8)]
        PRE, ST, OD, MISC = bank[0:2], bank[2:5], bank[5:7], bank[7]
        HB, YB = bank[2:5], bank[5:7]

        x_in = [sem(f"x_in{c}") for c in range(NC)]
        wkv_in, gate_in, w1_in, w2_in, wq_in, wo_in = map(sem, ("wkv_in", "gate_in", "w1_in", "w2_in", "wq_in", "wo_in"))
        consts, kdup, masked, summed, diag_ready = map(
            sem, ("consts", "kdup", "masked", "summed", "diag_ready"))
        ln_step, xn_ready, kl_ready, gate_step, comb_ready, y_added = map(
            sem, ("ln_step", "xn_ready", "kl_ready", "gate_step", "comb_ready", "y_added"))
        ql_ready, pre_used, max_ready, rec_ready, on_ready, att_added = map(
            sem, ("ql_ready", "pre_used", "max_ready", "rec_ready", "on_ready", "att_added"))
        std_ready, xnT_ready, kh_ready, v_ready, gexp_ready, h_ready = map(
            sem, ("std_ready", "xnT_ready", "kh_ready", "v_ready", "gexp_ready", "h_ready"))
        combT_ready, qh_ready, q_twice, row_ready, exp_ready = map(
            sem, ("combT_ready", "qh_ready", "q_twice", "row_ready", "exp_ready"))
        xT_done, k_done, v_done, lg_done, cT_done, h_done, y_done = map(
            sem, ("xT_done", "k_done", "v_done", "lg_done", "cT_done", "h_done", "y_done"))
        q_done, pre_done, row_done, st_done, pv_done, den_done, out_done = map(
            sem, ("q_done", "pre_done", "row_done", "st_done", "pv_done", "den_done", "out_done"))
        stored = sem("stored")

        def half(ap, r):
            return ap.rearrange("p (a r q) -> p r a q", a=2, r=2)[:, r]

        def pairs(ap):
            return ap.rearrange("p (a q) -> p a q", a=2)

        block = ctx.enter_context(nc.Block())

        @block.sync
        def _(sp):
            for c in range(NC):
                sp.dma_start(x_sb[:, CH * c:CH * c + CH, :],
                             x[W * c:W * c + W, :].rearrange("(t p) d -> p t d", p=P)).then_inc(x_in[c], 16)
            sp.dma_start(w1_sb[:, 0:E, :], w1.rearrange("e d f -> d e f")).then_inc(w1_in, 16)
            sp.dma_start(w1_sb[:, E, :], sw1).then_inc(w1_in, 16)
            sp.dma_start(b1_sb[:, :], b1T).then_inc(w1_in, 16)
            sp.dma_start(wo_sb[:, :, :], woT).then_inc(wo_in, 16)
            for t in range(NT):
                sp.wait_ge(att_added, KV * (t + 1))
                sp.dma_start(out[P * t:P * t + P, :], yacc[:, t, :]).then_inc(stored, 16)
            sp.wait_ge(stored, 16 * NT)

        @block.gpsimd
        def _(pool):
            pool.memset(ident[:, :], 0.0).then_inc(consts, 1)
            pool.memset(negident[:, :], 0.0).then_inc(consts, 1)
            pool.memset(ones[:, :], 1.0).then_inc(consts, 1)
            pool.memset(ones_r[:, :].bitcast(f32), 1.0).then_inc(consts, 1)
            pool.memset(causal[:, :], 0.0).then_inc(consts, 1)
            pool.memset(gp[:, :, :], -1.0).then_inc(consts, 1)
            pool.memset(comb[:, :, E:NE], 1.0).then_inc(consts, 1)
            pool.wait_ge(consts, 7)
            pool.memset(k_h1[HD:HD + 1, :, :].bitcast(f32), 1.0).then_inc(consts, 1)
            pool.wait_ge(consts, 8)
            pool.affine_select(out=ident[:, :], in_=ident[:, :], compare_op=ALU.not_equal, fill=1.0, base=0,
                               pattern=[[-1, P]], channel_multiplier=1).then_inc(consts, 1)
            pool.affine_select(out=negident[:, :], in_=negident[:, :], compare_op=ALU.not_equal, fill=-1.0, base=0,
                               pattern=[[-1, P]], channel_multiplier=1).then_inc(consts, 1)
            pool.affine_select(out=causal[:, W - P:W], in_=causal[:, W - P:W], compare_op=ALU.is_ge, fill=NEG, base=0,
                               pattern=[[-1, P]], channel_multiplier=1).then_inc(consts, 1)
            for n in range(2 * NC):
                c, p = n // 2, n % 2
                pool.wait_ge(kh_ready, 2 * n + 2)
                pool.tensor_copy(k_h1[0:HD, 2 * p:2 * p + 2, W * c:W * c + W],
                                 k_hl[0:HD, 2 * p:2 * p + 2, W * c:W * c + W]).then_inc(kdup, 1)

            def prepare(step):
                kind, g, h, c = step
                if kind == "M" and (h, c) == (REP - 1, len(max_chunks(g)) - 1):
                    pool.wait_ge(max_ready, g + 1)
                    if g >= 2:
                        pool.wait_ge(row_done, g - 1)
                    pool.tensor_tensor(diag[:, g % 2, :].rearrange("p (h q) -> p h q", h=REP),
                                       negident[:, None, :].broadcast_to([P, REP, P]),
                                       gmx[:, g % 2, :, None].broadcast_to([P, REP, P]),
                                       ALU.mult).then_inc(diag_ready, 1)

            for n in range(NF):
                for s in EARLY.get(n, []):
                    prepare(s)
            for u, (g, i, j) in enumerate(UNITS):
                here = pT[:, u % NP, :]
                pool.wait_ge(exp_ready, u + 1)
                if i == 0:
                    v = here.rearrange("p (h q) -> p h q", h=REP)
                    pool.affine_select(out=v, in_=v, compare_op=ALU.is_ge, fill=0.0, base=0,
                                       pattern=[[0, REP], [1, P]], channel_multiplier=-1).then_inc(masked, 1)
                if i == 0 and COUNT[g] == 1 or i == 1:
                    pool.wait_ge(masked, g + 1)
                    if g >= 2:
                        pool.wait_ge(den_done, g - 1)
                if i == 0 and COUNT[g] == 1:
                    pool.tensor_copy(acc[:, g % 2, :], here).then_inc(summed, 1)
                elif i == 1:
                    pool.tensor_tensor(acc[:, g % 2, :], pT[:, (u - 1) % NP, :], here, ALU.add).then_inc(summed, 1)
                elif i > 1:
                    pool.wait_ge(summed, ADDS[u - 1])
                    pool.tensor_tensor(acc[:, g % 2, :], acc[:, g % 2, :], here, ALU.add).then_inc(summed, 1)
                for s in steps_of(u):
                    prepare(s)

        @block.scalar
        def _(act):
            act.dma_start(wk_sb[:, :], wkT).then_inc(wkv_in, 16)
            act.dma_start(wv_sb[:, :], wvT).then_inc(wkv_in, 16)
            act.dma_start(gw_sb[:, :], gw).then_inc(gate_in, 16)
            act.dma_start(gb_sb[:, :], gb).then_inc(gate_in, 16)
            act.dma_start(w2_sb[:, 0:E, :], w2.rearrange("e f d -> f e d")).then_inc(w2_in, 16)
            act.dma_start(w2_sb[:, E, :], sw2).then_inc(w2_in, 16)
            act.dma_start(b2_sb[0:E, :], b2).then_inc(w2_in, 16)
            act.dma_start(b2_sb[E:NE, :], sb2).then_inc(w2_in, 16)
            act.dma_start(wq_sb[:, :], wqT).then_inc(wq_in, 16)

            act.wait_ge(ln_step, 3)
            nc.scalar.activation(std[:, :], vare[:, :], ACT.Sqrt).then_inc(std_ready, 1)
            for c in range(NC):
                act.wait_ge(xT_done, c + 1)
                nc.scalar.activation(xnT[:, W * c:W * c + W], bank[c % 2][:, :], ACT.Copy).then_inc(xnT_ready, 1)
                for p in range(2):
                    n = 2 * c + p
                    act.wait_ge(k_done, n + 1)
                    for r in range(2):
                        nc.scalar.activation(k_hl[0:HD, 2 * p + r, W * c:W * c + W],
                                             bank[2 + p][HD * r:HD * r + HD, :], ACT.Copy).then_inc(kh_ready, 1)
                for m in range(2):
                    n = 2 * c + m
                    act.wait_ge(v_done, n + 1)
                    nc.scalar.activation(v_sb[:, 2 * n:2 * n + 2, :],
                                         bank[4 + m][:, :].rearrange("p (t d) -> p t d", t=2),
                                         ACT.Copy).then_inc(v_ready, 1)
            act.wait_ge(gate_step, 2)
            nc.scalar.activation(gexp[:, :, :], lg[:, :, :], ACT.Exp).then_inc(gexp_ready, 1)

            def prepare(step):
                kind, g, h, c = step
                if kind == "C":
                    act.wait_ge(cT_done, g + 1)
                    nc.scalar.activation(combT[:, W * g:W * g + W], MISC[0:NE, :], ACT.Copy).then_inc(combT_ready, 1)
                if kind == "Q":
                    act.wait_ge(q_done, g + 1)
                    if g >= NQ:
                        act.wait_ge(st_done, LAST[g - NQ] + 1)
                    for r in range(2):
                        nc.scalar.activation(half(q_hh[0:HD, g % NQ, :], r),
                                             pairs(MISC[HD * r:HD * r + HD, 0:2 * P]), ACT.Copy).then_inc(qh_ready, 1)
                    act.wait_ge(qh_ready, 2 * (g + 1))
                    nc.scalar.activation(q_hh[HD:P, g % NQ, :], q_hh[0:HD, g % NQ, :].bitcast(f32),
                                         ACT.Copy).then_inc(q_twice, 1)
                if kind == "R":
                    act.wait_ge(row_done, g + 1)
                    if g >= NQ:
                        act.wait_ge(st_done, LAST[g - NQ] + 1)
                    nc.scalar.activation(q_lm[HD:HD + 1, g % NQ, :], MISC[HD:HD + 1, :], ACT.Copy).then_inc(row_ready, 1)

            act.wait_ge(w1_in, 48)
            for n in range(NF):
                act.wait_ge(h_done, n + 1)
                if n >= 3:
                    act.wait_ge(y_done, n - 2)
                nc.scalar.activation(hT[:, n % 3, :], HB[n % 3][:, :], ACT.Gelu,
                                     bias=b1_sb[:, n % NE:n % NE + 1]).then_inc(h_ready, 1)
                for s in EARLY.get(n, []):
                    prepare(s)
            for u, (g, i, j) in enumerate(UNITS):
                act.wait_ge(st_done, u + 1)
                if u >= NP:
                    act.wait_ge(pv_done, u - NP + 1)
                    act.wait_ge(summed, added(u - NP))
                nc.scalar.activation(pT[:, u % NP, :], ST[u % NST][:, :], ACT.Exp, scale=SCALE).then_inc(exp_ready, 1)
                for s in steps_of(u):
                    prepare(s)

        @block.vector
        def _(dve):
            for c in range(NC):
                dve.wait_ge(x_in[c], 16)
                for t in range(CH * c, CH * c + CH):
                    last = nc.vector.bn_stats(stats[:, t, :], x_sb[:, t, :])
            last.then_inc(ln_step, 1)
            dve.wait_ge(ln_step, 1)
            for t in range(NT):
                last = nc.vector.bn_aggr(mv[:, t, :], stats[:, t, :])
            last.then_inc(ln_step, 1)
            dve.wait_ge(ln_step, 2)
            nc.vector.tensor_scalar(vare[:, :], mv[:, :, 1], EPS, None, ALU.add).then_inc(ln_step, 1)
            dve.wait_ge(ln_step, 3)
            dve.wait_ge(std_ready, 1)
            nc.vector.reciprocal(r0[:, :], std[:, :]).then_inc(ln_step, 1)
            dve.wait_ge(ln_step, 4)
            nc.vector.tensor_tensor(r1[:, :], r0[:, :], r0[:, :], ALU.mult).then_inc(ln_step, 1)
            dve.wait_ge(ln_step, 5)
            nc.vector.tensor_tensor(rstd[:, :], r1[:, :], vare[:, :], ALU.mult).then_inc(ln_step, 1)
            dve.wait_ge(ln_step, 6)
            nc.vector.tensor_scalar(r1[:, :], rstd[:, :], -0.5, 1.5, ALU.mult, ALU.add).then_inc(ln_step, 1)
            dve.wait_ge(ln_step, 7)
            nc.vector.tensor_tensor(rstd[:, :], r0[:, :], r1[:, :], ALU.mult).then_inc(ln_step, 1)
            dve.wait_ge(ln_step, 8)
            for c in range(NC):
                for t in range(CH * c, CH * c + CH):
                    last = nc.vector.tensor_scalar(xn[:, t, :], x_sb[:, t, :], mv[:, t, 0:1], rstd[:, t:t + 1],
                                                   ALU.subtract, ALU.mult)
                last.then_inc(xn_ready, 1)
            for n in range(2 * NC):
                c, p = n // 2, n % 2
                dve.wait_ge(kh_ready, 2 * n + 2)
                for r in range(2):
                    k = 2 * p + r
                    last = nc.vector.tensor_tensor(k_hl[HD:P, k, W * c:W * c + W], bank[2 + p][HD * r:HD * r + HD, :],
                                                   k_hl[0:HD, k, W * c:W * c + W].bitcast(f32), ALU.subtract)
                last.then_inc(kl_ready, 1)
            dve.wait_ge(lg_done, 1)
            logits = bank[6][:, 0:NT * E].rearrange("p (t e) -> p t e", t=NT)
            nc.vector.reduce_max(gmax[:, :], logits, AX.X).then_inc(gate_step, 1)
            dve.wait_ge(gate_step, 1)
            nc.vector.tensor_tensor(lg[:, :, :], logits, gmax[:, :, None].broadcast_to([P, NT, E]),
                                    ALU.subtract).then_inc(gate_step, 1)
            dve.wait_ge(gexp_ready, 1)
            nc.vector.reduce_sum(gsum[:, :], gexp[:, :, :], AX.X).then_inc(gate_step, 1)
            dve.wait_ge(gate_step, 3)
            nc.vector.reciprocal(grec[:, :], gsum[:, :]).then_inc(gate_step, 1)
            dve.wait_ge(gate_step, 4)
            dve.wait_ge(consts, 8)
            nc.vector.tensor_tensor(gp[:, :, 0:E], gexp[:, :, :], grec[:, :, None].broadcast_to([P, NT, E]),
                                    ALU.mult).then_inc(gate_step, 1)
            dve.wait_ge(gate_step, 5)
            for t in range(NT):
                last = nc.vector.max(top[:, t, :], gp[:, t, 0:E])
            last.then_inc(gate_step, 1)
            dve.wait_ge(gate_step, 6)
            nc.vector.memset(top[:, :, 2:E], -1.0).then_inc(gate_step, 1)
            dve.wait_ge(gate_step, 7)
            for t in range(NT):
                last = nc.vector.match_replace(rest[:, t, :], top[:, t, :], gp[:, t, :], 0.0)
            last.then_inc(gate_step, 1)
            dve.wait_ge(gate_step, 8)
            nc.vector.tensor_tensor(comb[:, :, 0:E], gp[:, :, 0:E], rest[:, :, 0:E], ALU.subtract).then_inc(comb_ready, 1)
            dve.wait_ge(comb_ready, 1)

            def prepare(step):
                kind, g, h, c = step
                if kind == "Q":
                    dve.wait_ge(qh_ready, 2 * (g + 1))
                    if g >= NQ:
                        dve.wait_ge(st_done, LAST[g - NQ] + 1)
                    for r in range(2):
                        nc.vector.tensor_tensor(half(q_lm[0:HD, g % NQ, :], r),
                                                pairs(MISC[HD * r:HD * r + HD, 0:2 * P]),
                                                half(q_hh[0:HD, g % NQ, :].bitcast(f32), r),
                                                ALU.subtract).then_inc(ql_ready, 1)
                if kind == "M":
                    n, chunks = MORDER[step], max_chunks(g)
                    at, w = chunks[c]
                    dve.wait_ge(pre_done, n + 1)
                    if h == 0 and c == 0 and g >= 2:
                        dve.wait_ge(max_ready, g - 1)
                    src, dst = PRE[n % 2][:, 0:w], part[:, g % 2, h, c:c + 1]
                    if c < len(chunks) - 1:
                        nc.vector.reduce_max(dst, src, AX.X).then_inc(pre_used, 1)
                    else:
                        dve.wait_ge(pre_used, n)
                        nc.vector.tensor_tensor_reduce(out=junk[:, 0:w], in0=src, in1=causal[:, W - w:W], scale=1.0,
                                                       scalar=NEG, op0=ALU.add, op1=ALU.max,
                                                       accum_out=dst).then_inc(pre_used, 1)
                    if h == REP - 1 and c == len(chunks) - 1:
                        dve.wait_ge(pre_used, n + 1)
                        if g >= 2:
                            dve.wait_ge(diag_ready, g - 1)
                        nc.vector.reduce_max(gmx[:, g % 2, :], part[:, g % 2, :, 0:len(chunks)],
                                             AX.X).then_inc(max_ready, 1)

            dve.wait_ge(consts, 11)
            for n in range(NF + 1):
                if n:
                    m = n - 1
                    c, e = m // NE, m % NE
                    dve.wait_ge(y_done, m + 1)
                    if m:
                        dve.wait_ge(y_added, m)
                    for t in range(CH):
                        tile = CH * c + t
                        last = nc.vector.scalar_tensor_tensor(
                            out=yacc[:, tile, :], in0=YB[m % 2][:, P * t:P * t + P], scalar=comb[:, tile, e:e + 1],
                            in1=x_sb[:, tile, :] if e == 0 else yacc[:, tile, :], op0=ALU.mult, op1=ALU.add)
                    last.then_inc(y_added, 1)
                for s in EARLY.get(n, []):
                    prepare(s)
            dve.wait_ge(y_added, NF)

            for u in range(NU + 2 * LAG):
                for g in range(NG):
                    if LAST[g] == u - 2 * LAG:
                        qt = GROUPS[g][0]
                        dve.wait_ge(out_done, g + 1)
                        if g:
                            dve.wait_ge(att_added, g)
                        nc.vector.tensor_tensor(yacc[:, qt, :], OD[g % 2][:, 0:D], yacc[:, qt, :],
                                                ALU.add).then_inc(att_added, 1)
                for g in range(NG):
                    if LAST[g] == u - LAG:
                        dve.wait_ge(den_done, g + 1)
                        if g >= 2:
                            dve.wait_ge(on_ready, g - 1)
                        nc.vector.reciprocal(rec[:, g % 2, :], OD[g % 2][:, W // 2:W]).then_inc(rec_ready, 1)
                        dve.wait_ge(rec_ready, g + 1)
                        if g >= 2:
                            dve.wait_ge(out_done, g - 1)
                        nc.vector.tensor_tensor(on[:, g % 2, :], OD[g % 2][:, 0:W // 2], rec[:, g % 2, :],
                                                ALU.mult).then_inc(on_ready, 1)
                if u < NU:
                    for s in steps_of(u):
                        prepare(s)

        @block.tensor
        def _(pe):
            mm = nc.tensor.matmul
            pe.wait_ge(consts, 11)

            def transpose_x(c):
                pe.wait_ge(xn_ready, c + 1)
                if c >= 2:
                    pe.wait_ge(xnT_ready, c - 1)
                for t in range(CH):
                    last = nc.tensor.transpose(bank[c % 2][:, P * t:P * t + P], xn[:, CH * c + t, :], ident[:, :])
                last.then_inc(xT_done, 1)

            transpose_x(0)
            pe.wait_ge(wkv_in, 32)
            pe.wait_ge(gate_in, 32)
            for c in range(NC):
                if c + 1 < NC:
                    transpose_x(c + 1)
                pe.wait_ge(xnT_ready, c + 1)
                cols = xnT[:, W * c:W * c + W]
                for p in range(2):
                    if c:
                        pe.wait_ge(kl_ready, 2 * (c - 1) + p + 1)
                    mm(bank[2 + p][:, :], wk_sb[:, P * p:P * p + P], cols, start=True, stop=True).then_inc(k_done, 1)
                for m in range(2):
                    if c:
                        pe.wait_ge(v_ready, 2 * (c - 1) + m + 1)
                    for t in range(2):
                        tile = CH * c + 2 * m + t
                        last = mm(bank[4 + m][:, t * KV * HD:(t + 1) * KV * HD], xnT[:, P * tile:P * tile + P],
                                  wv_sb[:, :], start=True, stop=True)
                    last.then_inc(v_done, 1)
                for tile in range(CH * c, CH * c + CH):
                    dst = bank[6][:, E * tile:E * tile + E]
                    mm(dst, xnT[:, P * tile:P * tile + P], gw_sb[:, :], start=True, stop=False)
                    last = mm(dst, ones[0:1, :], gb_sb[:, :], start=False, stop=True)
            last.then_inc(lg_done, 1)

            def prepare(step):
                kind, g, h, c = step
                if kind == "C":
                    if g == 0:
                        pe.wait_ge(comb_ready, 1)
                    else:
                        pe.wait_ge(combT_ready, g)
                    for t in range(CH):
                        last = nc.tensor.transpose(MISC[0:NE, P * t:P * t + P], comb[:, CH * g + t, :], ident[:, :])
                    last.then_inc(cT_done, 1)
                if kind == "Q":
                    qt, kv = GROUPS[g]
                    pe.wait_ge(combT_ready, NC)
                    if g:
                        pe.wait_ge(ql_ready, 2 * g)
                    if g >= 3:
                        pe.wait_ge(row_ready, g - 1)
                    if g == 0:
                        pe.wait_ge(wq_in, 16)
                    for a in range(2):
                        pair = 2 * kv + a
                        last = mm(MISC[:, P * a:P * a + P], wq_sb[:, P * pair:P * pair + P],
                                  xnT[:, P * qt:P * qt + P], start=True, stop=True)
                    last.then_inc(q_done, 1)
                if kind == "M":
                    n = MORDER[step]
                    at, w = max_chunks(g)[c]
                    if h == 0 and c == 0:
                        pe.wait_ge(qh_ready, 2 * (g + 1))
                        pe.wait_ge(kdup, 2 * NC)
                    if n >= 2:
                        pe.wait_ge(pre_used, n - 1)
                    mm(PRE[n % 2][:, 0:w], q_hh[0:HD, g % NQ, P * h:P * h + P],
                       k_h1[0:HD, GROUPS[g][1], at:at + w], start=True, stop=True).then_inc(pre_done, 1)
                if kind == "R":
                    pe.wait_ge(diag_ready, g + 1)
                    pe.wait_ge(ql_ready, 2 * min(max(g + 2, 3), NG))
                    mm(MISC[0:HD + 1, :], ones_r[:, :], diag[:, g % 2, :], start=True, stop=True).then_inc(row_done, 1)

            pe.wait_ge(kl_ready, 2 * NC)
            pe.wait_ge(v_ready, 2 * NC)
            pe.wait_ge(gate_step, 2)
            pe.wait_ge(w1_in, 48)
            pe.wait_ge(w2_in, 64)
            for n in range(NF + 1):
                if n < NF:
                    c, e = n // NE, n % NE
                    if n >= 3:
                        pe.wait_ge(h_ready, n - 2)
                    mm(HB[n % 3][:, :], w1_sb[:, e, :], xnT[:, W * c:W * c + W], start=True,
                       stop=True).then_inc(h_done, 1)
                if n:
                    m = n - 1
                    c, e = m // NE, m % NE
                    pe.wait_ge(h_ready, m + 1)
                    if m >= 2:
                        pe.wait_ge(y_added, m - 1)
                    if e == E:
                        pe.wait_ge(combT_ready, c + 1)
                    for t in range(CH):
                        dst = YB[m % 2][:, P * t:P * t + P]
                        last = mm(dst, hT[:, m % 3, P * t:P * t + P], w2_sb[:, e, :], start=True, stop=e < E)
                        if e == E:
                            last = mm(dst, combT[:, P * (CH * c + t):P * (CH * c + t) + P], b2_sb[:, :], start=False,
                                      stop=True)
                    last.then_inc(y_done, 1)
                for s in EARLY.get(n, []):
                    prepare(s)

            pe.wait_ge(h_ready, NF)
            pe.wait_ge(y_added, NF)
            pe.wait_ge(wo_in, 16)
            for u in range(NU + 2 * LAG):
                if u < NU:
                    g, i, j = UNITS[u]
                    kv = GROUPS[g][1]
                    if i == 0:
                        pe.wait_ge(q_twice, g + 1)
                        pe.wait_ge(ql_ready, 2 * (g + 1))
                        pe.wait_ge(row_ready, g + 1)
                    if u >= NST:
                        pe.wait_ge(exp_ready, u - NST + 1)
                    dst, keys = ST[u % NST][:, :], slice(P * j, P * j + P)
                    mm(dst, k_hl[:, kv, keys], q_hh[:, g % NQ, :], start=True, stop=False)
                    mm(dst, k_h1[:, kv, keys], q_lm[:, g % NQ, :], start=False, stop=True).then_inc(st_done, 1)
                for g in range(NG):
                    if LAST[g] == u - 2 * LAG:
                        pe.wait_ge(on_ready, g + 1)
                        for a in range(2):
                            last = mm(OD[g % 2][:, 0:D], on[:, g % 2, P * a:P * a + P],
                                      wo_sb[:, 2 * GROUPS[g][1] + a, :], start=a == 0, stop=a == 1)
                        last.then_inc(out_done, 1)
                if 0 <= u - LAG < NU:
                    v = u - LAG
                    g, i, j = UNITS[v]
                    kv = GROUPS[g][1]
                    if i == 0:
                        pe.wait_ge(masked, g + 1)
                        if g >= 2:
                            pe.wait_ge(att_added, g - 1)
                    pe.wait_ge(exp_ready, v + 1)
                    for r in range(2):
                        last = mm(OD[g % 2][HD * r:HD * r + HD, 0:W // 2], v_sb[:, j, HD * kv:HD * kv + HD],
                                  pT[:, v % NP, W // 2 * r:W // 2 * (r + 1)], start=i == 0, stop=i == COUNT[g] - 1)
                    last.then_inc(pv_done, 1)
                    if v == LAST[g]:
                        pe.wait_ge(summed, ADDS[v])
                        for r in range(2):
                            last = mm(OD[g % 2][HD * r:HD * r + HD, W // 2:W], ones[:, 0:HD],
                                      acc[:, g % 2, W // 2 * r:W // 2 * (r + 1)], start=True, stop=True)
                        last.then_inc(den_done, 1)
                if u < NU:
                    for s in steps_of(u):
                        prepare(s)


def kernel(L0_attn_hidden_states, L0_attn_Wq, L0_attn_Wk, L0_attn_Wv, L0_attn_Wo, L0_ffn_gate_w, L0_ffn_gate_b,
           L0_ffn_sw1, L0_ffn_sb1, L0_ffn_sw2, L0_ffn_sb2, L0_ffn_w1, L0_ffn_b1, L0_ffn_w2, L0_ffn_b2):
    import numpy as np
    import concourse.bacc as bacc
    from concourse import mybir as mb
    from concourse.bass_utils import run_bass_kernel_spmd

    def a(v):
        return np.asarray(v)

    wo = a(L0_attn_Wo).T.reshape(KV, 2, 2, HD, D).transpose(1, 3, 0, 2, 4).reshape(P, H // 2, D)
    laid = {
        "x": a(L0_attn_hidden_states).reshape(S, D), "wqT": a(L0_attn_Wq).T, "wkT": a(L0_attn_Wk).T,
        "wvT": a(L0_attn_Wv).T, "woT": wo, "gw": a(L0_ffn_gate_w), "gb": a(L0_ffn_gate_b).reshape(1, E),
        "b1T": np.concatenate([a(L0_ffn_b1), a(L0_ffn_sb1)[None]]).T, "w1": a(L0_ffn_w1), "sw1": a(L0_ffn_sw1),
        "w2": a(L0_ffn_w2), "sw2": a(L0_ffn_sw2), "b2": a(L0_ffn_b2), "sb2": a(L0_ffn_sb2).reshape(1, D),
    }
    nc = bacc.Bacc("TRN2", target_bir_lowering=False, num_devices=1)
    arrays, args = {}, []
    for name, v in laid.items():
        v = np.ascontiguousarray(v)
        arrays[f"in_{name}"] = v
        args.append(nc.dram_tensor(f"in_{name}", v.shape, mb.dt.from_np(v.dtype), kind="ExternalInput").ap())
    out = nc.dram_tensor("out", (S, D), mb.dt.float32, kind="ExternalOutput").ap()
    layer(nc, *args, out)
    r = run_bass_kernel_spmd(nc, [arrays], core_ids=[0])
    return r.results[0]["out"].reshape(1, S, D)
```

```python
import concourse.bass as bass
from concourse import mybir
from contextlib import ExitStack

P = 128
S = 2048
D = 128
HD = 64
KV = 4
REP = 4
H = KV * REP
E = 8
NE = E + 1
NT = S // P
CH = 4
NC = NT // CH
W = CH * P
EPS = 1e-5
SCALE = HD ** -0.5
NEG = -1e30

NG = NT * KV
NQ = 4
NP = 10
NST = 2
NOD = 3
NM = 3
PAIR = 1
SUM = 2

ASCENDING = [(g // KV, g % KV) for g in range(NG)]
GROUPS = [x for pair in zip(ASCENDING[NG // 2:], ASCENDING[NG // 2 - 1::-1]) for x in pair]
UNITS = [(g, i, qt - i) for g, (qt, kv) in enumerate(GROUPS) for i in range(qt + 1)]
FIRST = [next(u for u, x in enumerate(UNITS) if x[0] == g) for g in range(NG)]
COUNT = [qt + 1 for qt, _ in GROUPS]
LAST = [FIRST[g] + COUNT[g] - 1 for g in range(NG)]
NU = len(UNITS)
PV = [u + 3 - u % 2 for u in range(NU)]
DEN = [PV[LAST[g]] + (2 if PV[LAST[g]] == LAST[g] + 2 else 0) for g in range(NG)]
REC = [u + 1 for u in DEN]
DIV = [u + 2 for u in DEN]
for g in range(1, NG):
    DIV[g] = max(DIV[g], DIV[g - 1] + 2)
PROJ = [u + 2 for u in DIV]
END = PROJ[-1] + 1
assert all(x == sorted(x) for x in (DEN, REC, DIV, PROJ))
assert all(PROJ[g] <= PV[FIRST[g + NOD]] for g in range(NG - NOD))


def max_chunks(g):
    left, at, out = COUNT[g] * P, 0, []
    while left:
        w = min(left, W)
        if left - w == P:
            w -= P
        out.append((at, w))
        at, left = at + w, left - w
    return out


def max_steps(g):
    return [("M", g, h, c) for h in range(REP) for c in range(len(max_chunks(g)))]


def steps_in(g):
    out = []
    for n in (g, g + 1):
        m = max_steps(n + 2) if n + 2 < NG else []
        r = [("R", n + 1, 0, 0)] if n + 1 < NG else []
        q = [("Q", n + 3, 0, 0)] if n + 3 < NG else []
        a, b = max(3, len(m) // 4), 3 * len(m) // 4
        out += m[:a] + r + m[a:b] + q + m[b:]
    return out


def steps_of(u):
    g = UNITS[u][0] // 2 * 2
    s, n, i = steps_in(g), COUNT[g] + COUNT[g + 1], u - FIRST[g]
    n = min(n, 2 * len(s))
    return s[len(s) * i // n:len(s) * (i + 1) // n]


def early(u):
    s = steps_of(u) if 0 <= u < NU else []
    return s[:len(s) // 2]


def late(u):
    s = steps_of(u) if 0 <= u < NU else []
    return s[len(s) // 2:]


SLOT = {s: u for u in range(NU) for s in steps_of(u)}
DIAG = {g: min(SLOT[("R", g, 0, 0)], max(SLOT[("R", g, 0, 0)] - 2, SLOT.get(max_steps(g)[-1], 0) + 1))
        for g in range(1, NG)}
assert all(SLOT[("Q", g + 4, 0, 0)] >= LAST[g] for g in range(NG - 4))


EARLY = {7: [("C", 0, 0, 0)], 8: [("C", 1, 0, 0)], 10: [("C", 2, 0, 0)], 12: [("C", 3, 0, 0)],
         18: [("Q", 0, 0, 0)], 20: [("Q", 1, 0, 0)], 22: [("Q", 2, 0, 0)],
         28: [("R", 0, 0, 0)]}
for n, (a, b) in enumerate(((20, 27), (28, 35))):
    m = max_steps(n)
    for k in range(a, b):
        EARLY[k] = EARLY.get(k, []) + m[len(m) * (k - a) // (b - a):len(m) * (k - a + 1) // (b - a)]
NF = NC * NE

STREAM = [s for n in range(NF) for s in EARLY.get(n, [])] + [s for u in range(NU) for s in steps_of(u)]
PREP = {s: n for n, s in enumerate(STREAM)}
MORDER = {s: n for n, s in enumerate(x for x in STREAM if x[0] == "M")}

def role(u):
    g, i, _ = UNITS[u]
    n = COUNT[g]
    if i == 0:
        return "only" if n == 1 else "wait"
    if i == 1:
        return "second"
    if i % 3 == 2:
        return "single" if i == n - 1 else "left"
    return "right" if i % 3 == 0 else "single"


def count(roles):
    out, n = [], 0
    for u in range(NU):
        n += role(u) in roles
        out.append(n)
    return out


ADDS = count(("only", "second", "right", "single"))
PAIRS = count(("right",))
RIGHTS = [u for u in range(NU) if role(u) == "right"]


def layer(nc, x, wqT, wkT, wvT, woT, gw, gb, b1T, w1, sw1, w2, sw2, b2, sb2, out):
    f32, f32r = mybir.dt.float32, mybir.dt.float32r
    ALU, ACT, AX = mybir.AluOpType, mybir.ActivationFunctionType, mybir.AxisListType

    ctx = ExitStack()
    with ctx:
        def sb(name, shape, dt=f32):
            return ctx.enter_context(nc.sbuf_tensor(name, shape, dt))

        def sem(name):
            return ctx.enter_context(nc.semaphore(name))

        wq_sb = sb("wq_sb", [P, H * HD])
        wk_sb = sb("wk_sb", [P, KV * HD])
        wv_sb = sb("wv_sb", [P, KV * HD])
        wo_sb = sb("wo_sb", [P, H // 2, D])
        gw_sb = sb("gw_sb", [P, E])
        gb_sb = sb("gb_sb", [1, E])
        w1_sb = sb("w1_sb", [P, NE, D])
        w2_sb = sb("w2_sb", [P, NE, D])
        b1_sb = sb("b1_sb", [P, NE])
        b2_sb = sb("b2_sb", [NE, D])
        ident = sb("ident", [P, P])
        negident = sb("negident", [P, P])
        ones = sb("ones", [P, P])
        ones_r = sb("ones_r", [P, HD + 1], f32r)
        causal = sb("causal", [P, W])
        x_sb = sb("x_sb", [P, NT, D])
        xn = sb("xn", [P, NT, D])
        xnT = sb("xnT", [P, S])
        stats = sb("stats", [P, NT, 6])
        mv = sb("mv", [P, NT, 2])
        vare = sb("vare", [P, NT])
        std = sb("std", [P, NT])
        r0 = sb("r0", [P, NT])
        r1 = sb("r1", [P, NT])
        rstd = sb("rstd", [P, NT])
        k_hl = sb("k_hl", [P, KV, S], f32r)
        k_h1 = sb("k_h1", [HD + 1, KV, S], f32r)
        v_sb = sb("v_sb", [P, NT, KV * HD])
        lg = sb("lg", [P, NT, E])
        gmax = sb("gmax", [P, NT])
        gexp = sb("gexp", [P, NT, E])
        gsum = sb("gsum", [P, NT])
        grec = sb("grec", [P, NT])
        gp = sb("gp", [P, NT, 2 * E])
        top = sb("top", [P, NT, E])
        rest = sb("rest", [P, NT, 2 * E])
        comb = sb("comb", [P, NT, NE])
        combT = sb("combT", [NE, S])
        hT = sb("hT", [P, 3, W])
        yacc = xn
        q_hh = sb("q_hh", [P, NQ, W], f32r)
        q_lm = sb("q_lm", [HD + 1, NQ, W], f32r)
        part = sb("part", [P, 2, REP, 4])
        gmx = sb("gmx", [P, 2, REP])
        diag = sb("diag", [P, 2, W], f32r)
        junk = sb("junk", [P, W])
        pT = sb("pT", [P, NP, W])
        acc = sb("acc", [P, 2, W])
        pair = sb("pair", [P, 2, W])
        logd = sb("logd", [P, W // 2])
        guess = sb("guess", [P, 2, W // 2])
        dr = sb("dr", [P, W // 2])
        minus = sb("minus", [P, W // 2])
        on = sb("on", [P, 2, W // 2])

        bank = [ctx.enter_context(nc.psum_tensor(f"bank{n}", [P, W], f32)) for n in range(8)]
        RING, ST, OD = (bank[0], bank[1], bank[7]), bank[2:4], bank[4:7]
        HB, YB = bank[2:5], bank[5:7]

        x_in = [sem(f"x_in{c}") for c in range(NC)]
        wkv_in, gate_in, w1_in, w2_in, wq_in, wo_in = map(sem, ("wkv_in", "gate_in", "w1_in", "w2_in", "wq_in", "wo_in"))
        consts, kdup, masked, summed = map(
            sem, ("consts", "kdup", "masked", "summed"))
        ln_step, xn_ready, kl_ready, gate_step, comb_ready, y_added = map(
            sem, ("ln_step", "xn_ready", "kl_ready", "gate_step", "comb_ready", "y_added"))
        ql_ready, pre_used, max_ready, paired, newton, on_ready, att_added = map(
            sem, ("ql_ready", "pre_used", "max_ready", "paired", "newton", "on_ready", "att_added"))
        diag_ready = sem("diag_ready")
        std_ready, xnT_ready, kh_ready, v_ready, gexp_ready, h_ready = map(
            sem, ("std_ready", "xnT_ready", "kh_ready", "v_ready", "gexp_ready", "h_ready"))
        combT_ready, qh_ready, q_twice, row_ready, exp_ready, logd_ready, guess_ready = map(
            sem, ("combT_ready", "qh_ready", "q_twice", "row_ready", "exp_ready", "logd_ready", "guess_ready"))
        xT_done, k_done, v_done, lg_done, cT_done, h_done, y_done = map(
            sem, ("xT_done", "k_done", "v_done", "lg_done", "cT_done", "h_done", "y_done"))
        q_done, pre_done, row_done, st_done, pv_done, den_done, out_done = map(
            sem, ("q_done", "pre_done", "row_done", "st_done", "pv_done", "den_done", "out_done"))
        stored = sem("stored")

        def half(ap, r):
            return ap.rearrange("p (a r q) -> p r a q", a=2, r=2)[:, r]

        def ring(step):
            return RING[PREP[step] % NM]

        def pairs(ap):
            return ap.rearrange("p (a q) -> p a q", a=2)

        block = ctx.enter_context(nc.Block())

        @block.sync
        def _(sp):
            for c in range(NC):
                sp.dma_start(x_sb[:, CH * c:CH * c + CH, :],
                             x[W * c:W * c + W, :].rearrange("(t p) d -> p t d", p=P)).then_inc(x_in[c], 16)
            sp.dma_start(w1_sb[:, 0:E, :], w1.rearrange("e d f -> d e f")).then_inc(w1_in, 16)
            sp.dma_start(w1_sb[:, E, :], sw1).then_inc(w1_in, 16)
            sp.dma_start(b1_sb[:, :], b1T).then_inc(w1_in, 16)
            sp.dma_start(wo_sb[:, :, :], woT).then_inc(wo_in, 16)
            for t in sorted(range(NT), key=lambda t: GROUPS.index((t, KV - 1))):
                sp.wait_ge(att_added, max(GROUPS.index((t, kv)) for kv in range(KV)) + 1)
                sp.dma_start(out[P * t:P * t + P, :], yacc[:, t, :]).then_inc(stored, 16)
            sp.wait_ge(stored, 16 * NT)

        @block.gpsimd
        def _(pool):
            pool.memset(ident[:, :], 0.0).then_inc(consts, 1)
            pool.memset(negident[:, :], 0.0).then_inc(consts, 1)
            pool.memset(ones[:, :], 1.0).then_inc(consts, 1)
            pool.memset(ones_r[:, :].bitcast(f32), 1.0).then_inc(consts, 1)
            pool.memset(causal[:, :], 0.0).then_inc(consts, 1)
            pool.memset(gp[:, :, :], -1.0).then_inc(consts, 1)
            pool.memset(comb[:, :, E:NE], 1.0).then_inc(consts, 1)
            pool.wait_ge(consts, 7)
            pool.memset(k_h1[HD:HD + 1, :, :].bitcast(f32), 1.0).then_inc(consts, 1)
            pool.wait_ge(consts, 8)
            pool.affine_select(out=ident[:, :], in_=ident[:, :], compare_op=ALU.not_equal, fill=1.0, base=0,
                               pattern=[[-1, P]], channel_multiplier=1).then_inc(consts, 1)
            pool.affine_select(out=negident[:, :], in_=negident[:, :], compare_op=ALU.not_equal, fill=-1.0, base=0,
                               pattern=[[-1, P]], channel_multiplier=1).then_inc(consts, 1)
            pool.affine_select(out=causal[:, W - P:W], in_=causal[:, W - P:W], compare_op=ALU.is_ge, fill=NEG, base=0,
                               pattern=[[-1, P]], channel_multiplier=1).then_inc(consts, 1)
            for n in range(2 * NC):
                c, p = n // 2, n % 2
                pool.wait_ge(kh_ready, 2 * n + 2)
                pool.tensor_copy(k_h1[0:HD, 2 * p:2 * p + 2, W * c:W * c + W],
                                 k_hl[0:HD, 2 * p:2 * p + 2, W * c:W * c + W]).then_inc(kdup, 1)

            def add(u):
                g, what = UNITS[u][0], role(u)
                here, total = pT[:, u % NP, :], acc[:, g % 2, :]
                if what == "right":
                    pool.wait_ge(paired, PAIRS[u])
                else:
                    pool.wait_ge(exp_ready, u + 1)
                if what in ("only", "second"):
                    pool.wait_ge(masked, g + 1)
                    if g >= 2:
                        pool.wait_ge(den_done, g - 1)
                if what == "only":
                    pool.tensor_copy(total, here).then_inc(summed, 1)
                elif what == "second":
                    pool.tensor_tensor(total, pT[:, (u - 1) % NP, :], here, ALU.add).then_inc(summed, 1)
                elif what in ("right", "single"):
                    pool.wait_ge(summed, ADDS[u - 1])
                    pool.tensor_tensor(total, total, pair[:, PAIRS[u] % 2, :] if what == "right" else here,
                                       ALU.add).then_inc(summed, 1)

            for u in range(NU + SUM):
                v = u - 1
                if 0 <= v < NU and UNITS[v][1] == 0:
                    pool.wait_ge(exp_ready, v + 1)
                    p = pT[:, v % NP, :].rearrange("p (h q) -> p h q", h=REP)
                    pool.affine_select(out=p, in_=p, compare_op=ALU.is_ge, fill=0.0, base=0,
                                       pattern=[[0, REP], [1, P]], channel_multiplier=-1).then_inc(masked, 1)
                if 0 <= u - SUM < NU:
                    add(u - SUM)

        @block.scalar
        def _(act):
            act.dma_start(wk_sb[:, :], wkT).then_inc(wkv_in, 16)
            act.dma_start(wv_sb[:, :], wvT).then_inc(wkv_in, 16)
            act.dma_start(gw_sb[:, :], gw).then_inc(gate_in, 16)
            act.dma_start(gb_sb[:, :], gb).then_inc(gate_in, 16)
            act.dma_start(w2_sb[:, 0:E, :], w2.rearrange("e f d -> f e d")).then_inc(w2_in, 16)
            act.dma_start(w2_sb[:, E, :], sw2).then_inc(w2_in, 16)
            act.dma_start(b2_sb[0:E, :], b2).then_inc(w2_in, 16)
            act.dma_start(b2_sb[E:NE, :], sb2).then_inc(w2_in, 16)
            act.dma_start(wq_sb[:, :], wqT).then_inc(wq_in, 16)

            act.wait_ge(ln_step, 3)
            nc.scalar.activation(std[:, :], vare[:, :], ACT.Sqrt).then_inc(std_ready, 1)
            for c in range(NC):
                act.wait_ge(xT_done, c + 1)
                nc.scalar.activation(xnT[:, W * c:W * c + W], bank[c % 2][:, :], ACT.Copy).then_inc(xnT_ready, 1)
                for p in range(2):
                    n = 2 * c + p
                    act.wait_ge(k_done, n + 1)
                    for r in range(2):
                        nc.scalar.activation(k_hl[0:HD, 2 * p + r, W * c:W * c + W],
                                             bank[2 + p][HD * r:HD * r + HD, :], ACT.Copy).then_inc(kh_ready, 1)
                for m in range(2):
                    n = 2 * c + m
                    act.wait_ge(v_done, n + 1)
                    nc.scalar.activation(v_sb[:, 2 * n:2 * n + 2, :],
                                         bank[4 + m][:, :].rearrange("p (t d) -> p t d", t=2),
                                         ACT.Copy).then_inc(v_ready, 1)
            act.wait_ge(gate_step, 2)
            nc.scalar.activation(gexp[:, :, :], lg[:, :, :], ACT.Exp).then_inc(gexp_ready, 1)

            def prepare(step):
                kind, g, h, c = step
                if kind == "C":
                    act.wait_ge(cT_done, g + 1)
                    nc.scalar.activation(combT[:, W * g:W * g + W], ring(step)[0:NE, :], ACT.Copy).then_inc(combT_ready, 1)
                if kind == "Q":
                    act.wait_ge(q_done, g + 1)
                    if g >= NQ:
                        act.wait_ge(st_done, LAST[g - NQ] + 1)
                    for r in range(2):
                        nc.scalar.activation(half(q_hh[0:HD, g % NQ, :], r),
                                             pairs(ring(step)[HD * r:HD * r + HD, 0:2 * P]), ACT.Copy).then_inc(qh_ready, 1)
                    act.wait_ge(qh_ready, 2 * (g + 1))
                    nc.scalar.activation(q_hh[HD:P, g % NQ, :], q_hh[0:HD, g % NQ, :].bitcast(f32),
                                         ACT.Copy).then_inc(q_twice, 1)
                if kind == "R":
                    act.wait_ge(row_done, g + 1)
                    if g >= NQ:
                        act.wait_ge(st_done, LAST[g - NQ] + 1)
                    nc.scalar.activation(q_lm[HD:HD + 1, g % NQ, :], ring(step)[HD:HD + 1, :], ACT.Copy).then_inc(row_ready, 1)

            def build_diag(g):
                act.wait_ge(max_ready, g + 1)
                if g >= 2:
                    act.wait_ge(row_done, g - 1)
                for h in range(REP):
                    last = nc.scalar.activation(diag[:, g % 2, P * h:P * h + P], negident[:, :], ACT.Copy,
                                                scale=gmx[:, g % 2, h:h + 1])
                last.then_inc(diag_ready, 1)

            act.wait_ge(w1_in, 48)
            for n in range(NF):
                act.wait_ge(h_done, n + 1)
                if n >= 3:
                    act.wait_ge(y_done, n - 2)
                nc.scalar.activation(hT[:, n % 3, :], HB[n % 3][:, :], ACT.Gelu,
                                     bias=b1_sb[:, n % NE:n % NE + 1]).then_inc(h_ready, 1)
                for s in EARLY.get(n, []):
                    prepare(s)
                    if s == max_steps(0)[-1]:
                        build_diag(0)
            nc.scalar.preload_act_table_set("natural_log_exp_and_others")
            for u in range(END):
                for g in range(NG):
                    if REC[g] == u:
                        act.wait_ge(den_done, g + 1)
                        if g:
                            act.wait_ge(guess_ready, g)
                        nc.scalar.activation(logd[:, :], OD[g % NOD][:, W // 2:W], ACT.Ln).then_inc(logd_ready, 1)
                        act.wait_ge(logd_ready, g + 1)
                        if g >= 2:
                            act.wait_ge(newton, 2 * (g - 1))
                        nc.scalar.activation(guess[:, g % 2, :], logd[:, :], ACT.Exp, scale=-1.0).then_inc(guess_ready, 1)
                if u >= NU:
                    continue
                act.wait_ge(st_done, u + 1)
                if u >= NP:
                    act.wait_ge(pv_done, u - NP + 1)
                    v = u - NP
                    what = role(v)
                    if what in ("left", "right"):
                        act.wait_ge(paired, PAIRS[v + 1] if what == "left" else PAIRS[v])
                    else:
                        act.wait_ge(summed, ADDS[v + 1] if what == "wait" else ADDS[v])
                nc.scalar.activation(pT[:, u % NP, :], ST[u % NST][:, :], ACT.Exp, scale=SCALE).then_inc(exp_ready, 1)
                for g in range(1, NG):
                    if DIAG[g] == u:
                        build_diag(g)
                for s in steps_of(u):
                    prepare(s)

        @block.vector
        def _(dve):
            for c in range(NC):
                dve.wait_ge(x_in[c], 16)
                for t in range(CH * c, CH * c + CH):
                    last = nc.vector.bn_stats(stats[:, t, :], x_sb[:, t, :])
            last.then_inc(ln_step, 1)
            dve.wait_ge(ln_step, 1)
            for t in range(NT):
                last = nc.vector.bn_aggr(mv[:, t, :], stats[:, t, :])
            last.then_inc(ln_step, 1)
            dve.wait_ge(ln_step, 2)
            nc.vector.tensor_scalar(vare[:, :], mv[:, :, 1], EPS, None, ALU.add).then_inc(ln_step, 1)
            dve.wait_ge(ln_step, 3)
            dve.wait_ge(std_ready, 1)
            nc.vector.reciprocal(r0[:, :], std[:, :]).then_inc(ln_step, 1)
            dve.wait_ge(ln_step, 4)
            nc.vector.tensor_tensor(r1[:, :], r0[:, :], r0[:, :], ALU.mult).then_inc(ln_step, 1)
            dve.wait_ge(ln_step, 5)
            nc.vector.tensor_tensor(rstd[:, :], r1[:, :], vare[:, :], ALU.mult).then_inc(ln_step, 1)
            dve.wait_ge(ln_step, 6)
            nc.vector.tensor_scalar(r1[:, :], rstd[:, :], -0.5, 1.5, ALU.mult, ALU.add).then_inc(ln_step, 1)
            dve.wait_ge(ln_step, 7)
            nc.vector.tensor_tensor(rstd[:, :], r0[:, :], r1[:, :], ALU.mult).then_inc(ln_step, 1)
            dve.wait_ge(ln_step, 8)
            for c in range(NC):
                for t in range(CH * c, CH * c + CH):
                    last = nc.vector.tensor_scalar(xn[:, t, :], x_sb[:, t, :], mv[:, t, 0:1], rstd[:, t:t + 1],
                                                   ALU.subtract, ALU.mult)
                last.then_inc(xn_ready, 1)
            for n in range(2 * NC):
                c, p = n // 2, n % 2
                dve.wait_ge(kh_ready, 2 * n + 2)
                for r in range(2):
                    k = 2 * p + r
                    last = nc.vector.tensor_tensor(k_hl[HD:P, k, W * c:W * c + W], bank[2 + p][HD * r:HD * r + HD, :],
                                                   k_hl[0:HD, k, W * c:W * c + W].bitcast(f32), ALU.subtract)
                last.then_inc(kl_ready, 1)
            dve.wait_ge(lg_done, 1)
            logits = bank[6][:, 0:NT * E].rearrange("p (t e) -> p t e", t=NT)
            nc.vector.reduce_max(gmax[:, :], logits, AX.X).then_inc(gate_step, 1)
            dve.wait_ge(gate_step, 1)
            nc.vector.tensor_tensor(lg[:, :, :], logits, gmax[:, :, None].broadcast_to([P, NT, E]),
                                    ALU.subtract).then_inc(gate_step, 1)
            dve.wait_ge(gexp_ready, 1)
            nc.vector.reduce_sum(gsum[:, :], gexp[:, :, :], AX.X).then_inc(gate_step, 1)
            dve.wait_ge(gate_step, 3)
            nc.vector.reciprocal(grec[:, :], gsum[:, :]).then_inc(gate_step, 1)
            dve.wait_ge(gate_step, 4)
            dve.wait_ge(consts, 8)
            nc.vector.tensor_tensor(gp[:, :, 0:E], gexp[:, :, :], grec[:, :, None].broadcast_to([P, NT, E]),
                                    ALU.mult).then_inc(gate_step, 1)
            dve.wait_ge(gate_step, 5)
            for t in range(NT):
                last = nc.vector.max(top[:, t, :], gp[:, t, 0:E])
            last.then_inc(gate_step, 1)
            dve.wait_ge(gate_step, 6)
            nc.vector.memset(top[:, :, 2:E], -1.0).then_inc(gate_step, 1)
            dve.wait_ge(gate_step, 7)
            for t in range(NT):
                last = nc.vector.match_replace(rest[:, t, :], top[:, t, :], gp[:, t, :], 0.0)
            last.then_inc(gate_step, 1)
            dve.wait_ge(gate_step, 8)
            nc.vector.tensor_tensor(comb[:, :, 0:E], gp[:, :, 0:E], rest[:, :, 0:E], ALU.subtract).then_inc(comb_ready, 1)
            dve.wait_ge(comb_ready, 1)

            def prepare_q(step):
                kind, g, h, c = step
                if kind == "Q":
                    dve.wait_ge(qh_ready, 2 * (g + 1))
                    if g >= NQ:
                        dve.wait_ge(st_done, LAST[g - NQ] + 1)
                    for r in range(2):
                        nc.vector.tensor_tensor(half(q_lm[0:HD, g % NQ, :], r),
                                                pairs(ring(step)[HD * r:HD * r + HD, 0:2 * P]),
                                                half(q_hh[0:HD, g % NQ, :].bitcast(f32), r),
                                                ALU.subtract).then_inc(ql_ready, 1)

            def prepare(step):
                kind, g, h, c = step
                if kind == "M":
                    n, chunks = MORDER[step], max_chunks(g)
                    at, w = chunks[c]
                    dve.wait_ge(pre_done, n + 1)
                    if h == 0 and c == 0 and g >= 2:
                        dve.wait_ge(max_ready, g - 1)
                    src, dst = ring(step)[:, 0:w], part[:, g % 2, h, c:c + 1]
                    if c < len(chunks) - 1:
                        nc.vector.reduce_max(dst, src, AX.X).then_inc(pre_used, 1)
                    else:
                        dve.wait_ge(pre_used, n)
                        nc.vector.tensor_tensor_reduce(out=junk[:, 0:w], in0=src, in1=causal[:, W - w:W], scale=1.0,
                                                       scalar=NEG, op0=ALU.add, op1=ALU.max,
                                                       accum_out=dst).then_inc(pre_used, 1)
                    if h == REP - 1 and c == len(chunks) - 1:
                        dve.wait_ge(pre_used, n + 1)
                        if g >= 2:
                            dve.wait_ge(diag_ready, g - 1)
                        nc.vector.reduce_max(gmx[:, g % 2, :], part[:, g % 2, :, 0:len(chunks)],
                                             AX.X).then_inc(max_ready, 1)

            dve.wait_ge(consts, 11)
            for n in range(NF + 1):
                if n:
                    m = n - 1
                    c, e = m // NE, m % NE
                    dve.wait_ge(y_done, m + 1)
                    if m:
                        dve.wait_ge(y_added, m)
                    for t in range(CH):
                        tile = CH * c + t
                        last = nc.vector.scalar_tensor_tensor(
                            out=yacc[:, tile, :], in0=YB[m % 2][:, P * t:P * t + P], scalar=comb[:, tile, e:e + 1],
                            in1=x_sb[:, tile, :] if e == 0 else yacc[:, tile, :], op0=ALU.mult, op1=ALU.add)
                    last.then_inc(y_added, 1)
                for s in EARLY.get(n, []):
                    prepare_q(s)
                    prepare(s)
            dve.wait_ge(y_added, NF)

            for u in range(END):
                for s in late(u - 1):
                    prepare(s)
                v = u - PAIR
                if 0 <= v < NU and role(v) == "right":
                    dve.wait_ge(exp_ready, v + 1)
                    if PAIRS[v] > 2:
                        dve.wait_ge(summed, ADDS[RIGHTS[PAIRS[v] - 3]])
                    nc.vector.tensor_tensor(pair[:, PAIRS[v] % 2, :], pT[:, (v - 1) % NP, :], pT[:, v % NP, :],
                                            ALU.add).then_inc(paired, 1)
                for g in range(NG):
                    if DIV[g] == u:
                        dve.wait_ge(guess_ready, g + 1)
                        r = guess[:, g % 2, :]
                        nc.vector.tensor_tensor(dr[:, :], OD[g % NOD][:, W // 2:W], r, ALU.mult).then_inc(newton, 1)
                        dve.wait_ge(newton, 2 * g + 1)
                        nc.vector.scalar_tensor_tensor(out=minus[:, :], in0=dr[:, :], scalar=2.0, in1=r,
                                                       op0=ALU.subtract, op1=ALU.mult).then_inc(newton, 1)
                        dve.wait_ge(newton, 2 * g + 2)
                        if g >= 2:
                            dve.wait_ge(out_done, g - 1)
                        nc.vector.scalar_tensor_tensor(out=on[:, g % 2, :], in0=OD[g % NOD][:, 0:W // 2], scalar=-1.0,
                                                       in1=minus[:, :], op0=ALU.mult, op1=ALU.mult).then_inc(on_ready, 1)
                for g in range(NG):
                    if PROJ[g] == u:
                        qt = GROUPS[g][0]
                        dve.wait_ge(out_done, g + 1)
                        if g:
                            dve.wait_ge(att_added, g)
                        nc.vector.tensor_tensor(yacc[:, qt, :], OD[g % NOD][:, 0:D], yacc[:, qt, :],
                                                ALU.add).then_inc(att_added, 1)
                for s in early(u - 1) + late(u - 1):
                    prepare_q(s)
                for s in early(u):
                    prepare(s)

        @block.tensor
        def _(pe):
            mm = nc.tensor.matmul
            pe.wait_ge(consts, 11)

            def transpose_x(c):
                pe.wait_ge(xn_ready, c + 1)
                if c >= 2:
                    pe.wait_ge(xnT_ready, c - 1)
                for t in range(CH):
                    last = nc.tensor.transpose(bank[c % 2][:, P * t:P * t + P], xn[:, CH * c + t, :], ident[:, :])
                last.then_inc(xT_done, 1)

            transpose_x(0)
            pe.wait_ge(wkv_in, 32)
            pe.wait_ge(gate_in, 32)
            for c in range(NC):
                if c + 1 < NC:
                    transpose_x(c + 1)
                pe.wait_ge(xnT_ready, c + 1)
                cols = xnT[:, W * c:W * c + W]
                for p in range(2):
                    if c:
                        pe.wait_ge(kl_ready, 2 * (c - 1) + p + 1)
                    mm(bank[2 + p][:, :], wk_sb[:, P * p:P * p + P], cols, start=True, stop=True).then_inc(k_done, 1)
                for m in range(2):
                    if c:
                        pe.wait_ge(v_ready, 2 * (c - 1) + m + 1)
                    for t in range(2):
                        tile = CH * c + 2 * m + t
                        last = mm(bank[4 + m][:, t * KV * HD:(t + 1) * KV * HD], xnT[:, P * tile:P * tile + P],
                                  wv_sb[:, :], start=True, stop=True)
                    last.then_inc(v_done, 1)
                for tile in range(CH * c, CH * c + CH):
                    dst = bank[6][:, E * tile:E * tile + E]
                    mm(dst, xnT[:, P * tile:P * tile + P], gw_sb[:, :], start=True, stop=False)
                    last = mm(dst, ones[0:1, :], gb_sb[:, :], start=False, stop=True)
            last.then_inc(lg_done, 1)

            def prepare(step):
                kind, g, h, c = step
                if PREP[step] >= NM:
                    before = STREAM[PREP[step] - NM]
                    if before[0] == "M":
                        pe.wait_ge(pre_used, MORDER[before] + 1)
                    if before[0] == "Q":
                        pe.wait_ge(ql_ready, 2 * (before[1] + 1))
                    if before[0] == "R":
                        pe.wait_ge(row_ready, before[1] + 1)
                    if before[0] == "C":
                        pe.wait_ge(combT_ready, before[1] + 1)
                if kind == "C":
                    if g == 0:
                        pe.wait_ge(comb_ready, 1)
                    for t in range(CH):
                        last = nc.tensor.transpose(ring(step)[0:NE, P * t:P * t + P], comb[:, CH * g + t, :], ident[:, :])
                    last.then_inc(cT_done, 1)
                if kind == "Q":
                    qt, kv = GROUPS[g]
                    if g == 0:
                        pe.wait_ge(wq_in, 16)
                    for a in range(2):
                        pair = 2 * kv + a
                        last = mm(ring(step)[:, P * a:P * a + P], wq_sb[:, P * pair:P * pair + P],
                                  xnT[:, P * qt:P * qt + P], start=True, stop=True)
                    last.then_inc(q_done, 1)
                if kind == "M":
                    at, w = max_chunks(g)[c]
                    if h == 0 and c == 0:
                        pe.wait_ge(qh_ready, 2 * (g + 1))
                        pe.wait_ge(kdup, 2 * NC)
                    mm(ring(step)[:, 0:w], q_hh[0:HD, g % NQ, P * h:P * h + P],
                       k_h1[0:HD, GROUPS[g][1], at:at + w], start=True, stop=True).then_inc(pre_done, 1)
                if kind == "R":
                    pe.wait_ge(diag_ready, g + 1)
                    mm(ring(step)[0:HD + 1, :], ones_r[:, :], diag[:, g % 2, :], start=True, stop=True).then_inc(row_done, 1)

            pe.wait_ge(kl_ready, 2 * NC)
            pe.wait_ge(v_ready, 2 * NC)
            pe.wait_ge(gate_step, 2)
            pe.wait_ge(w1_in, 48)
            pe.wait_ge(w2_in, 64)
            for n in range(NF + 1):
                if n < NF:
                    c, e = n // NE, n % NE
                    if n >= 3:
                        pe.wait_ge(h_ready, n - 2)
                    mm(HB[n % 3][:, :], w1_sb[:, e, :], xnT[:, W * c:W * c + W], start=True,
                       stop=True).then_inc(h_done, 1)
                if n:
                    m = n - 1
                    c, e = m // NE, m % NE
                    pe.wait_ge(h_ready, m + 1)
                    if m >= 2:
                        pe.wait_ge(y_added, m - 1)
                    if e == E:
                        pe.wait_ge(combT_ready, c + 1)
                    for t in range(CH):
                        dst = YB[m % 2][:, P * t:P * t + P]
                        last = mm(dst, hT[:, m % 3, P * t:P * t + P], w2_sb[:, e, :], start=True, stop=e < E)
                        if e == E:
                            last = mm(dst, combT[:, P * (CH * c + t):P * (CH * c + t) + P], b2_sb[:, :], start=False,
                                      stop=True)
                    last.then_inc(y_done, 1)
                for s in EARLY.get(n, []):
                    prepare(s)

            pe.wait_ge(h_ready, NF)
            pe.wait_ge(y_added, NF)
            pe.wait_ge(wo_in, 16)
            for u in range(END):
                if u < NU:
                    g, i, j = UNITS[u]
                    kv = GROUPS[g][1]
                    if i == 0:
                        pe.wait_ge(q_twice, g + 1)
                        pe.wait_ge(ql_ready, 2 * (g + 1))
                        pe.wait_ge(row_ready, g + 1)
                    if u >= NST:
                        pe.wait_ge(exp_ready, u - NST + 1)
                    dst, keys = ST[u % NST][:, :], slice(P * j, P * j + P)
                    mm(dst, k_hl[:, kv, keys], q_hh[:, g % NQ, :], start=True, stop=False)
                    mm(dst, k_h1[:, kv, keys], q_lm[:, g % NQ, :], start=False, stop=True).then_inc(st_done, 1)
                for s in early(u):
                    prepare(s)
                for g in range(NG):
                    if PROJ[g] == u:
                        pe.wait_ge(on_ready, g + 1)
                        for a in range(2):
                            last = mm(OD[g % NOD][:, 0:D], on[:, g % 2, P * a:P * a + P],
                                      wo_sb[:, 2 * GROUPS[g][1] + a, :], start=a == 0, stop=a == 1)
                        last.then_inc(out_done, 1)
                for v in range(max(u - 3, 0), min(u, NU)):
                    if PV[v] != u:
                        continue
                    g, i, j = UNITS[v]
                    kv = GROUPS[g][1]
                    if i == 0:
                        pe.wait_ge(masked, g + 1)
                        if g >= NOD:
                            pe.wait_ge(att_added, g - NOD + 1)
                    pe.wait_ge(exp_ready, v + 1)
                    for r in range(2):
                        last = mm(OD[g % NOD][HD * r:HD * r + HD, 0:W // 2], v_sb[:, j, HD * kv:HD * kv + HD],
                                  pT[:, v % NP, W // 2 * r:W // 2 * (r + 1)], start=i == 0, stop=i == COUNT[g] - 1)
                    last.then_inc(pv_done, 1)
                for g in range(NG):
                    if DEN[g] == u:
                        pe.wait_ge(summed, ADDS[LAST[g]])
                        for r in range(2):
                            last = mm(OD[g % NOD][HD * r:HD * r + HD, W // 2:W], ones[:, 0:HD],
                                      acc[:, g % 2, W // 2 * r:W // 2 * (r + 1)], start=True, stop=True)
                        last.then_inc(den_done, 1)
                for s in late(u):
                    prepare(s)


def kernel(L0_attn_hidden_states, L0_attn_Wq, L0_attn_Wk, L0_attn_Wv, L0_attn_Wo, L0_ffn_gate_w, L0_ffn_gate_b,
           L0_ffn_sw1, L0_ffn_sb1, L0_ffn_sw2, L0_ffn_sb2, L0_ffn_w1, L0_ffn_b1, L0_ffn_w2, L0_ffn_b2):
    import numpy as np
    import concourse.bacc as bacc
    from concourse import mybir as mb
    from concourse.bass_utils import run_bass_kernel_spmd

    def a(v):
        return np.asarray(v)

    wo = a(L0_attn_Wo).T.reshape(KV, 2, 2, HD, D).transpose(1, 3, 0, 2, 4).reshape(P, H // 2, D)
    laid = {
        "x": a(L0_attn_hidden_states).reshape(S, D), "wqT": a(L0_attn_Wq).T, "wkT": a(L0_attn_Wk).T,
        "wvT": a(L0_attn_Wv).T, "woT": wo, "gw": a(L0_ffn_gate_w), "gb": a(L0_ffn_gate_b).reshape(1, E),
        "b1T": np.concatenate([a(L0_ffn_b1), a(L0_ffn_sb1)[None]]).T, "w1": a(L0_ffn_w1), "sw1": a(L0_ffn_sw1),
        "w2": a(L0_ffn_w2), "sw2": a(L0_ffn_sw2), "b2": a(L0_ffn_b2), "sb2": a(L0_ffn_sb2).reshape(1, D),
    }
    nc = bacc.Bacc("TRN2", target_bir_lowering=False, num_devices=1)
    arrays, args = {}, []
    for name, v in laid.items():
        v = np.ascontiguousarray(v)
        arrays[f"in_{name}"] = v
        args.append(nc.dram_tensor(f"in_{name}", v.shape, mb.dt.from_np(v.dtype), kind="ExternalInput").ap())
    out = nc.dram_tensor("out", (S, D), mb.dt.float32, kind="ExternalOutput").ap()
    layer(nc, *args, out)
    r = run_bass_kernel_spmd(nc, [arrays], core_ids=[0])
    return r.results[0]["out"].reshape(1, S, D)
```

```python
import concourse.bass as bass
from concourse import mybir
from contextlib import ExitStack

P = 128
S = 2048
D = 128
HD = 64
KV = 4
REP = 4
H = KV * REP
E = 8
NE = E + 1
NT = S // P
CH = 4
NC = NT // CH
W = CH * P
EPS = 1e-5
LNPARTS = (slice(0, CH), slice(CH, NT))
LN = 8
SCALE = HD ** -0.5
NEG = -1e30

NG = NT * KV
NQ = 4
NP = 10
NST = 2
NOD = 3
NM = 3
BATCH = 2
PAIR = 1
SUM = 2

ASCENDING = [(g // KV, g % KV) for g in range(NG)]
GROUPS = [x for pair in zip(ASCENDING[NG // 2:], ASCENDING[NG // 2 - 1::-1]) for x in pair]
UNITS = [(g, i, qt - i) for g, (qt, kv) in enumerate(GROUPS) for i in range(qt + 1)]
FIRST = [next(u for u, x in enumerate(UNITS) if x[0] == g) for g in range(NG)]
COUNT = [qt + 1 for qt, _ in GROUPS]
LAST = [FIRST[g] + COUNT[g] - 1 for g in range(NG)]
NU = len(UNITS)


def batched(u):
    return u + (-1 - u) % BATCH


PV = [batched(u + 2) for u in range(NU)]
DEN = [batched(LAST[g] + 4) for g in range(NG)]
REC = [u + 1 for u in DEN]
DIV = [u + 2 for u in DEN]
for g in range(1, NG):
    DIV[g] = max(DIV[g], DIV[g - 1] + 2)
PROJ = [u + 3 for u in DIV]
END = PROJ[-1] + 1
assert all(x == sorted(x) for x in (DEN, REC, DIV, PROJ))
assert all(DEN[g] >= PV[LAST[g]] for g in range(NG))
assert all(PROJ[g] <= PV[FIRST[g + NOD]] for g in range(NG - NOD))


def max_chunks(g):
    left, at, out = COUNT[g] * P, 0, []
    while left:
        w = min(left, W)
        if left - w == P:
            w -= P
        out.append((at, w))
        at, left = at + w, left - w
    return out


def max_steps(g):
    return [("M", g, h, c) for h in range(REP) for c in range(len(max_chunks(g)))]


def steps_in(g):
    out = []
    for n in (g, g + 1):
        m = max_steps(n + 2) if n + 2 < NG else []
        r = [("R", n + 1, 0, 0)] if n + 1 < NG else []
        q = [("Q", n + 3, 0, 0)] if n + 3 < NG else []
        a, b = max(3, len(m) // 3), 3 * len(m) // 4
        out += m[:a] + r + m[a:b] + q + m[b:]
    return out


def steps_of(u):
    g = UNITS[u][0] // 2 * 2
    s, n, i = steps_in(g), COUNT[g] + COUNT[g + 1], u - FIRST[g]
    n = min(n, 2 * len(s))
    return s[len(s) * i // n:len(s) * (i + 1) // n]


def early(u):
    s = steps_of(u) if 0 <= u < NU else []
    return s[:len(s) // 2]


def late(u):
    s = steps_of(u) if 0 <= u < NU else []
    return s[len(s) // 2:]


SLOT = {s: u for u in range(NU) for s in steps_of(u)}
DIAG = {g: min(SLOT[("R", g, 0, 0)], max(SLOT[("R", g, 0, 0)] - 2, SLOT.get(max_steps(g)[-1], 0) + 1))
        for g in range(2, NG)}
assert all(SLOT[("Q", g + 4, 0, 0)] >= LAST[g] for g in range(NG - 4))


EARLY = {7: [("C", 0, 0, 0)], 8: [("C", 1, 0, 0)], 10: [("C", 2, 0, 0)], 12: [("C", 3, 0, 0)],
         15: [("Q", 0, 0, 0)], 17: [("Q", 1, 0, 0)], 19: [("Q", 2, 0, 0)],
         29: [("R", 0, 0, 0)]}
EARLY_DIAG = {27: 0, 34: 1}

for n, (a, b) in enumerate(((18, 26), (26, 33))):
    m = max_steps(n)
    for k in range(a, b):
        EARLY[k] = EARLY.get(k, []) + m[len(m) * (k - a) // (b - a):len(m) * (k - a + 1) // (b - a)]
NF = NC * NE

STREAM = [s for n in range(NF) for s in EARLY.get(n, [])] + [s for u in range(NU) for s in steps_of(u)]
PREP = {s: n for n, s in enumerate(STREAM)}
MORDER = {s: n for n, s in enumerate(x for x in STREAM if x[0] == "M")}

def role(u):
    g, i, _ = UNITS[u]
    n = COUNT[g]
    if i == 0:
        return "only" if n == 1 else "wait"
    if i == 1:
        return "second"
    if i % 3 == 2:
        return "single" if i == n - 1 else "left"
    return "right" if i % 3 == 0 else "single"


def count(roles):
    out, n = [], 0
    for u in range(NU):
        n += role(u) in roles
        out.append(n)
    return out


ADDS = count(("only", "second", "right", "single"))
PAIRS = count(("right",))
RIGHTS = [u for u in range(NU) if role(u) == "right"]


def layer(nc, x, wqT, wkT, wvT, woT, gw, gb, b1T, w1, sw1, w2, sw2, b2, sb2, out):
    f32, f32r = mybir.dt.float32, mybir.dt.float32r
    ALU, ACT, AX = mybir.AluOpType, mybir.ActivationFunctionType, mybir.AxisListType

    ctx = ExitStack()
    with ctx:
        def sb(name, shape, dt=f32):
            return ctx.enter_context(nc.sbuf_tensor(name, shape, dt))

        def sem(name):
            return ctx.enter_context(nc.semaphore(name))

        wq_sb = sb("wq_sb", [P, H * HD])
        wk_sb = sb("wk_sb", [P, KV * HD])
        wvg_sb = sb("wvg_sb", [P, KV * HD + E])
        wo_sb = sb("wo_sb", [P, H // 2, D])
        gb_sb = sb("gb_sb", [P, E])
        w1_sb = sb("w1_sb", [P, NE, D])
        w2_sb = sb("w2_sb", [P, NE, D])
        b1_sb = sb("b1_sb", [P, NE])
        b2_sb = sb("b2_sb", [NE, D])
        ident = sb("ident", [P, P])
        negident = sb("negident", [P, P])
        ones = sb("ones", [P, P])
        ones_r = sb("ones_r", [P, HD + 1], f32r)
        causal = sb("causal", [P, W])
        x_sb = sb("x_sb", [P, NT, D])
        xn = sb("xn", [P, NT, D])
        xnT = sb("xnT", [P, S])
        stats = sb("stats", [P, NT, 6])
        mv = sb("mv", [P, NT, 2])
        vare = sb("vare", [P, NT])
        std = sb("std", [P, NT])
        r0 = sb("r0", [P, NT])
        r1 = sb("r1", [P, NT])
        rstd = sb("rstd", [P, NT])
        k_hl = sb("k_hl", [P, KV, S], f32r)
        k_h1 = sb("k_h1", [HD + 1, KV, S], f32r)
        v_sb = sb("v_sb", [P, NT, KV * HD])
        lg = sb("lg", [P, NT, E])
        gexp = sb("gexp", [P, NT, E])
        gmax = sb("gmax", [P, NT])
        gsum = sb("gsum", [P, NT])
        grec = sb("grec", [P, NT])
        gp = sb("gp", [P, NT, 2 * E])
        top = sb("top", [P, NT, E])
        rest = sb("rest", [P, NT, 2 * E])
        comb = sb("comb", [P, NT, NE])
        combT = sb("combT", [NE, S])
        hT = sb("hT", [P, 3, W])
        yacc = xn
        q_hh = sb("q_hh", [P, NQ, W], f32r)
        q_lm = sb("q_lm", [HD + 1, NQ, W], f32r)
        part = sb("part", [P, 2, REP, 4])
        gmx = sb("gmx", [P, 2, REP])
        diag = sb("diag", [P, 2, W], f32r)
        junk = sb("junk", [P, W])
        pT = sb("pT", [P, NP, W])
        acc = sb("acc", [P, 2, W])
        pair = sb("pair", [P, 2, W])
        logd = sb("logd", [P, W // 2])
        guess = sb("guess", [P, 2, W // 2])
        dr = sb("dr", [P, W // 2])
        minus = sb("minus", [P, W // 2])
        on = sb("on", [P, 2, W // 2])

        bank = [ctx.enter_context(nc.psum_tensor(f"bank{n}", [P, W], f32)) for n in range(8)]
        RING, ST, OD = (bank[0], bank[1], bank[7]), bank[2:4], bank[4:7]
        HB, YB = (bank[4], bank[2], bank[3]), bank[5:7]

        x_in = [sem(f"x_in{c}") for c in range(NC)]
        wkv_in, gate_in, w1_in, w2_in, wq_in, wo_in = map(sem, ("wkv_in", "gate_in", "w1_in", "w2_in", "wq_in", "wo_in"))
        consts, kdup, masked, summed = map(
            sem, ("consts", "kdup", "masked", "summed"))
        ln_step, xn_ready, kl_ready, lg_ready, gate_step, comb_ready, y_added = map(
            sem, ("ln_step", "xn_ready", "kl_ready", "lg_ready", "gate_step", "comb_ready", "y_added"))
        ql_ready, pre_used, max_ready, paired, newton, on_ready, att_added = map(
            sem, ("ql_ready", "pre_used", "max_ready", "paired", "newton", "on_ready", "att_added"))
        diag_ready = sem("diag_ready")
        std_ready, xnT_ready, kh_ready, v_ready, gexp_ready, h_ready = map(
            sem, ("std_ready", "xnT_ready", "kh_ready", "v_ready", "gexp_ready", "h_ready"))
        combT_ready, qh_ready, q_twice, row_ready, exp_ready, logd_ready, guess_ready = map(
            sem, ("combT_ready", "qh_ready", "q_twice", "row_ready", "exp_ready", "logd_ready", "guess_ready"))
        xT_done, k_done, v_done, cT_done, h_done, y_done = map(
            sem, ("xT_done", "k_done", "v_done", "cT_done", "h_done", "y_done"))
        q_done, pre_done, row_done, st_done, pv_done, den_done, out_done = map(
            sem, ("q_done", "pre_done", "row_done", "st_done", "pv_done", "den_done", "out_done"))
        stored = sem("stored")

        def hidden(n):
            return (bank[4], bank[0], bank[1])[n] if n < 3 else HB[n % 3]

        def half(ap, r):
            return ap.rearrange("p (a r q) -> p r a q", a=2, r=2)[:, r]

        def ring(step):
            return RING[PREP[step] % NM]

        def pairs(ap):
            return ap.rearrange("p (a q) -> p a q", a=2)

        block = ctx.enter_context(nc.Block())

        @block.sync
        def _(sp):
            for c in range(NC):
                sp.dma_start(x_sb[:, CH * c:CH * c + CH, :],
                             x[W * c:W * c + W, :].rearrange("(t p) d -> p t d", p=P)).then_inc(x_in[c], 16)
            sp.dma_start(w1_sb[:, 0:E, :], w1.rearrange("e d f -> d e f")).then_inc(w1_in, 16)
            sp.dma_start(w1_sb[:, E, :], sw1).then_inc(w1_in, 16)
            sp.dma_start(b1_sb[:, :], b1T).then_inc(w1_in, 16)
            sp.dma_start(gb_sb[:, :], gb).then_inc(gate_in, 16)
            sp.dma_start(w2_sb[:, 0:E, :], w2.rearrange("e f d -> f e d")).then_inc(w2_in, 16)
            sp.dma_start(w2_sb[:, E, :], sw2).then_inc(w2_in, 16)
            sp.dma_start(b2_sb[0:E, :], b2).then_inc(w2_in, 16)
            sp.dma_start(b2_sb[E:NE, :], sb2).then_inc(w2_in, 16)
            sp.dma_start(wq_sb[:, :], wqT).then_inc(wq_in, 16)
            sp.dma_start(wo_sb[:, :, :], woT).then_inc(wo_in, 16)
            for t in sorted(range(NT), key=lambda t: GROUPS.index((t, KV - 1))):
                sp.wait_ge(att_added, max(GROUPS.index((t, kv)) for kv in range(KV)) + 1)
                sp.dma_start(out[P * t:P * t + P, :], yacc[:, t, :]).then_inc(stored, 16)
            sp.wait_ge(stored, 16 * NT)

        @block.gpsimd
        def _(pool):
            pool.memset(ident[:, :], 0.0).then_inc(consts, 1)
            pool.memset(negident[:, :], 0.0).then_inc(consts, 1)
            pool.memset(ones[:, :], 1.0).then_inc(consts, 1)
            pool.memset(ones_r[:, :].bitcast(f32), 1.0).then_inc(consts, 1)
            pool.memset(causal[:, :], 0.0).then_inc(consts, 1)
            pool.memset(gp[:, :, :], -1.0).then_inc(consts, 1)
            pool.memset(comb[:, :, E:NE], 1.0).then_inc(consts, 1)
            pool.wait_ge(consts, 7)
            pool.affine_select(out=ident[:, :], in_=ident[:, :], compare_op=ALU.not_equal, fill=1.0, base=0,
                               pattern=[[-1, P]], channel_multiplier=1).then_inc(consts, 1)
            pool.affine_select(out=negident[:, :], in_=negident[:, :], compare_op=ALU.not_equal, fill=-1.0, base=0,
                               pattern=[[-1, P]], channel_multiplier=1).then_inc(consts, 1)
            pool.affine_select(out=causal[:, W - P:W], in_=causal[:, W - P:W], compare_op=ALU.is_ge, fill=NEG, base=0,
                               pattern=[[-1, P]], channel_multiplier=1).then_inc(consts, 1)
            pool.wait_ge(consts, 10)
            pool.memset(k_h1[HD:HD + 1, :, :].bitcast(f32), 1.0).then_inc(kdup, 1)
            pool.wait_ge(kdup, 1)
            for n in range(2 * NC):
                c, p = n // 2, n % 2
                pool.wait_ge(kh_ready, 2 * n + 2)
                pool.tensor_copy(k_h1[0:HD, 2 * p:2 * p + 2, W * c:W * c + W],
                                 k_hl[0:HD, 2 * p:2 * p + 2, W * c:W * c + W]).then_inc(kdup, 1)

            def add(u):
                g, what = UNITS[u][0], role(u)
                here, total = pT[:, u % NP, :], acc[:, g % 2, :]
                if what == "right":
                    pool.wait_ge(paired, PAIRS[u])
                else:
                    pool.wait_ge(exp_ready, u + 1)
                if what in ("only", "second"):
                    pool.wait_ge(masked, g + 1)
                    if g >= 2:
                        pool.wait_ge(den_done, g - 1)
                if what == "only":
                    pool.tensor_copy(total, here).then_inc(summed, 1)
                elif what == "second":
                    pool.tensor_tensor(total, pT[:, (u - 1) % NP, :], here, ALU.add).then_inc(summed, 1)
                elif what in ("right", "single"):
                    pool.wait_ge(summed, ADDS[u - 1])
                    pool.tensor_tensor(total, total, pair[:, PAIRS[u] % 2, :] if what == "right" else here,
                                       ALU.add).then_inc(summed, 1)

            for u in range(NU + SUM):
                v = u - 1
                if 0 <= v < NU and UNITS[v][1] == 0:
                    pool.wait_ge(exp_ready, v + 1)
                    p = pT[:, v % NP, :].rearrange("p (h q) -> p h q", h=REP)
                    pool.affine_select(out=p, in_=p, compare_op=ALU.is_ge, fill=0.0, base=0,
                                       pattern=[[0, REP], [1, P]], channel_multiplier=-1).then_inc(masked, 1)
                if 0 <= u - SUM < NU:
                    add(u - SUM)

        @block.scalar
        def _(act):
            nc.scalar.preload_act_table_set("sqrt_and_others")
            act.dma_start(wvg_sb[:, 0:KV * HD], wvT).then_inc(wkv_in, 16)
            act.dma_start(wvg_sb[:, KV * HD:], gw).then_inc(wkv_in, 16)
            act.dma_start(wk_sb[:, :], wkT).then_inc(wkv_in, 16)


            def deviations(k):
                act.wait_ge(ln_step, LN * k + 3)
                tiles = LNPARTS[k]
                nc.scalar.activation(std[:, tiles], vare[:, tiles], ACT.Sqrt).then_inc(std_ready, 1)

            def copy_x(c):
                act.wait_ge(xT_done, c + 1)
                nc.scalar.activation(xnT[:, W * c:W * c + W], bank[c % 2][:, :], ACT.Copy).then_inc(xnT_ready, 1)

            deviations(0)
            copy_x(0)
            deviations(1)
            for c in range(NC):
                for tile in range(CH * c, CH * c + CH):
                    if tile == NT - 1:
                        nc.scalar.preload_act_table_set("exp_and_others")
                    act.wait_ge(v_done, tile + 1)
                    nc.scalar.activation(v_sb[:, tile, :], bank[4 + tile % CH][:, 0:KV * HD],
                                         ACT.Copy).then_inc(v_ready, 1)
                if c + 1 < NC:
                    copy_x(c + 1)
                else:
                    act.wait_ge(gate_step, 2)
                    nc.scalar.activation(gexp[:, :, :], lg[:, :, :], ACT.Exp).then_inc(gexp_ready, 1)
                for p in range(2):
                    n = 2 * c + p
                    act.wait_ge(k_done, n + 1)
                    for r in range(2):
                        nc.scalar.activation(k_hl[0:HD, 2 * p + r, W * c:W * c + W],
                                             bank[2 + p][HD * r:HD * r + HD, :], ACT.Copy).then_inc(kh_ready, 1)
            nc.scalar.preload_act_table_set("gelu_and_others")

            def prepare(step):
                kind, g, h, c = step
                if kind == "C":
                    act.wait_ge(cT_done, g + 1)
                    nc.scalar.activation(combT[:, W * g:W * g + W], ring(step)[0:NE, :], ACT.Copy).then_inc(combT_ready, 1)
                if kind == "Q":
                    act.wait_ge(q_done, g + 1)
                    if g >= NQ:
                        act.wait_ge(st_done, LAST[g - NQ] + 1)
                    for r in range(2):
                        nc.scalar.activation(half(q_hh[0:HD, g % NQ, :], r),
                                             pairs(ring(step)[HD * r:HD * r + HD, 0:2 * P]), ACT.Copy).then_inc(qh_ready, 1)
                    act.wait_ge(qh_ready, 2 * (g + 1))
                    nc.scalar.activation(q_hh[HD:P, g % NQ, :], q_hh[0:HD, g % NQ, :].bitcast(f32),
                                         ACT.Copy).then_inc(q_twice, 1)
                if kind == "R":
                    act.wait_ge(row_done, g + 1)
                    if g >= NQ:
                        act.wait_ge(st_done, LAST[g - NQ] + 1)
                    nc.scalar.activation(q_lm[HD:HD + 1, g % NQ, :], ring(step)[HD:HD + 1, :], ACT.Copy).then_inc(row_ready, 1)

            def build_diag(g):
                act.wait_ge(max_ready, g + 1)
                if g >= 2:
                    act.wait_ge(row_done, g - 1)
                for h in range(REP):
                    last = nc.scalar.activation(diag[:, g % 2, P * h:P * h + P], negident[:, :], ACT.Copy,
                                                scale=gmx[:, g % 2, h:h + 1])
                last.then_inc(diag_ready, 1)

            act.wait_ge(w1_in, 48)
            for n in range(NF):
                act.wait_ge(h_done, n + 1)
                if n >= 3:
                    act.wait_ge(y_done, n - 2)
                nc.scalar.activation(hT[:, n % 3, :], hidden(n)[:, :], ACT.Gelu,
                                     bias=b1_sb[:, n % NE:n % NE + 1]).then_inc(h_ready, 1)
                for s in EARLY.get(n, []):
                    prepare(s)
                if n in EARLY_DIAG:
                    build_diag(EARLY_DIAG[n])
            nc.scalar.preload_act_table_set("natural_log_exp_and_others")
            for u in range(END):
                for g in range(NG):
                    if REC[g] == u:
                        act.wait_ge(den_done, g + 1)
                        if g:
                            act.wait_ge(guess_ready, g)
                        nc.scalar.activation(logd[:, :], OD[g % NOD][:, W // 2:W], ACT.Ln).then_inc(logd_ready, 1)
                        act.wait_ge(logd_ready, g + 1)
                        if g >= 2:
                            act.wait_ge(newton, 2 * (g - 1))
                        nc.scalar.activation(guess[:, g % 2, :], logd[:, :], ACT.Exp, scale=-1.0).then_inc(guess_ready, 1)
                if u >= NU:
                    continue
                act.wait_ge(st_done, u + 1)
                if u >= NP:
                    act.wait_ge(pv_done, u - NP + 1)
                    v = u - NP
                    what = role(v)
                    if what in ("left", "right"):
                        act.wait_ge(paired, PAIRS[v + 1] if what == "left" else PAIRS[v])
                    else:
                        act.wait_ge(summed, ADDS[v + 1] if what == "wait" else ADDS[v])
                nc.scalar.activation(pT[:, u % NP, :], ST[u % NST][:, :], ACT.Exp, scale=SCALE).then_inc(exp_ready, 1)
                for g in range(2, NG):
                    if DIAG[g] == u:
                        build_diag(g)
                for s in steps_of(u):
                    prepare(s)

        @block.vector
        def _(dve):
            def statistics(c):
                dve.wait_ge(x_in[c], 16)
                for t in range(CH * c, CH * c + CH):
                    last = nc.vector.bn_stats(stats[:, t, :], x_sb[:, t, :])
                return last

            def variances(k):
                tiles = LNPARTS[k]
                dve.wait_ge(ln_step, LN * k + 1)
                for t in range(tiles.start, tiles.stop):
                    last = nc.vector.bn_aggr(mv[:, t, :], stats[:, t, :])
                last.then_inc(ln_step, 1)
                dve.wait_ge(ln_step, LN * k + 2)
                nc.vector.tensor_scalar(vare[:, tiles], mv[:, tiles, 1], EPS, None, ALU.add).then_inc(ln_step, 1)

            def factors(k):
                tiles = LNPARTS[k]
                dve.wait_ge(ln_step, LN * k + 3)
                dve.wait_ge(std_ready, k + 1)
                nc.vector.reciprocal(r0[:, tiles], std[:, tiles]).then_inc(ln_step, 1)
                dve.wait_ge(ln_step, LN * k + 4)
                nc.vector.tensor_tensor(r1[:, tiles], r0[:, tiles], r0[:, tiles], ALU.mult).then_inc(ln_step, 1)
                dve.wait_ge(ln_step, LN * k + 5)
                nc.vector.tensor_tensor(rstd[:, tiles], r1[:, tiles], vare[:, tiles], ALU.mult).then_inc(ln_step, 1)
                dve.wait_ge(ln_step, LN * k + 6)
                nc.vector.tensor_scalar(r1[:, tiles], rstd[:, tiles], -0.5, 1.5, ALU.mult, ALU.add).then_inc(ln_step, 1)
                dve.wait_ge(ln_step, LN * k + 7)
                nc.vector.tensor_tensor(rstd[:, tiles], r0[:, tiles], r1[:, tiles], ALU.mult).then_inc(ln_step, 1)

            def normalise(c):
                for t in range(CH * c, CH * c + CH):
                    last = nc.vector.tensor_scalar(xn[:, t, :], x_sb[:, t, :], mv[:, t, 0:1], rstd[:, t:t + 1],
                                                   ALU.subtract, ALU.mult)
                last.then_inc(xn_ready, 1)

            statistics(0).then_inc(ln_step, 1)
            variances(0)
            statistics(1)
            factors(0)
            dve.wait_ge(ln_step, LN)
            normalise(0)
            statistics(2)
            statistics(3).then_inc(ln_step, 1)
            variances(1)
            factors(1)
            dve.wait_ge(ln_step, 2 * LN)
            for c in range(1, NC):
                normalise(c)
            def gate():
                dve.wait_ge(lg_ready, NT)
                nc.vector.reduce_max(gmax[:, :], lg[:, :, :], AX.X).then_inc(gate_step, 1)
                dve.wait_ge(gate_step, 1)
                nc.vector.tensor_tensor(lg[:, :, :], lg[:, :, :], gmax[:, :, None].broadcast_to([P, NT, E]),
                                        ALU.subtract).then_inc(gate_step, 1)
                dve.wait_ge(gexp_ready, 1)
                nc.vector.reduce_sum(gsum[:, :], gexp[:, :, :], AX.X).then_inc(gate_step, 1)
                dve.wait_ge(gate_step, 3)
                nc.vector.reciprocal(grec[:, :], gsum[:, :]).then_inc(gate_step, 1)
                dve.wait_ge(gate_step, 4)
                dve.wait_ge(consts, 7)
                nc.vector.tensor_tensor(gp[:, :, 0:E], gexp[:, :, :], grec[:, :, None].broadcast_to([P, NT, E]),
                                        ALU.mult).then_inc(gate_step, 1)
                dve.wait_ge(gate_step, 5)
                for t in range(NT):
                    last = nc.vector.max(top[:, t, :], gp[:, t, 0:E])
                last.then_inc(gate_step, 1)
                dve.wait_ge(gate_step, 6)
                nc.vector.memset(top[:, :, 2:E], -1.0).then_inc(gate_step, 1)
                dve.wait_ge(gate_step, 7)
                for t in range(NT):
                    last = nc.vector.match_replace(rest[:, t, :], top[:, t, :], gp[:, t, :], 0.0)
                last.then_inc(gate_step, 1)
                dve.wait_ge(gate_step, 8)
                nc.vector.tensor_tensor(comb[:, :, 0:E], gp[:, :, 0:E], rest[:, :, 0:E], ALU.subtract).then_inc(comb_ready, 1)

            dve.wait_ge(gate_in, 16)
            for c in range(NC):
                for tile in range(CH * c, CH * c + CH):
                    dve.wait_ge(v_ready, tile + 1)
                    nc.vector.tensor_tensor(lg[:, tile, :], bank[4 + tile % CH][:, KV * HD:KV * HD + E], gb_sb[:, :],
                                            ALU.add).then_inc(lg_ready, 1)
                if c == NC - 1:
                    gate()
                for p in range(2):
                    dve.wait_ge(kh_ready, 2 * (2 * c + p) + 2)
                    for r in range(2):
                        k = 2 * p + r
                        last = nc.vector.tensor_tensor(k_hl[HD:P, k, W * c:W * c + W], bank[2 + p][HD * r:HD * r + HD, :],
                                                       k_hl[0:HD, k, W * c:W * c + W].bitcast(f32), ALU.subtract)
                    last.then_inc(kl_ready, 1)
            dve.wait_ge(comb_ready, 1)

            def prepare_q(step):
                kind, g, h, c = step
                if kind == "Q":
                    dve.wait_ge(qh_ready, 2 * (g + 1))
                    if g >= NQ:
                        dve.wait_ge(st_done, LAST[g - NQ] + 1)
                    for r in range(2):
                        nc.vector.tensor_tensor(half(q_lm[0:HD, g % NQ, :], r),
                                                pairs(ring(step)[HD * r:HD * r + HD, 0:2 * P]),
                                                half(q_hh[0:HD, g % NQ, :].bitcast(f32), r),
                                                ALU.subtract).then_inc(ql_ready, 1)

            def prepare(step):
                kind, g, h, c = step
                if kind == "M":
                    n, chunks = MORDER[step], max_chunks(g)
                    at, w = chunks[c]
                    dve.wait_ge(pre_done, n + 1)
                    if h == 0 and c == 0 and g >= 2:
                        dve.wait_ge(max_ready, g - 1)
                    src, dst = ring(step)[:, 0:w], part[:, g % 2, h, c:c + 1]
                    if c < len(chunks) - 1:
                        nc.vector.reduce_max(dst, src, AX.X).then_inc(pre_used, 1)
                    else:
                        dve.wait_ge(pre_used, n)
                        nc.vector.tensor_tensor_reduce(out=junk[:, 0:w], in0=src, in1=causal[:, W - w:W], scale=1.0,
                                                       scalar=NEG, op0=ALU.add, op1=ALU.max,
                                                       accum_out=dst).then_inc(pre_used, 1)
                    if h == REP - 1 and c == len(chunks) - 1:
                        dve.wait_ge(pre_used, n + 1)
                        if g >= 2:
                            dve.wait_ge(diag_ready, g - 1)
                        nc.vector.reduce_max(gmx[:, g % 2, :], part[:, g % 2, :, 0:len(chunks)],
                                             AX.X).then_inc(max_ready, 1)

            dve.wait_ge(consts, 10)
            for n in range(NF + 1):
                if n:
                    m = n - 1
                    c, e = m // NE, m % NE
                    dve.wait_ge(y_done, m + 1)
                    if m:
                        dve.wait_ge(y_added, m)
                    for t in range(CH):
                        tile = CH * c + t
                        last = nc.vector.scalar_tensor_tensor(
                            out=yacc[:, tile, :], in0=YB[m % 2][:, P * t:P * t + P], scalar=comb[:, tile, e:e + 1],
                            in1=x_sb[:, tile, :] if e == 0 else yacc[:, tile, :], op0=ALU.mult, op1=ALU.add)
                    last.then_inc(y_added, 1)
                for s in EARLY.get(n, []):
                    prepare_q(s)
                    prepare(s)
            dve.wait_ge(y_added, NF)

            for u in range(END):
                for s in late(u - 1):
                    prepare(s)
                v = u - PAIR
                if 0 <= v < NU and role(v) == "right":
                    dve.wait_ge(exp_ready, v + 1)
                    if PAIRS[v] > 2:
                        dve.wait_ge(summed, ADDS[RIGHTS[PAIRS[v] - 3]])
                    nc.vector.tensor_tensor(pair[:, PAIRS[v] % 2, :], pT[:, (v - 1) % NP, :], pT[:, v % NP, :],
                                            ALU.add).then_inc(paired, 1)
                for g in range(NG):
                    if DIV[g] == u:
                        dve.wait_ge(guess_ready, g + 1)
                        r = guess[:, g % 2, :]
                        nc.vector.tensor_tensor(dr[:, :], OD[g % NOD][:, W // 2:W], r, ALU.mult).then_inc(newton, 1)
                        dve.wait_ge(newton, 2 * g + 1)
                        nc.vector.scalar_tensor_tensor(out=minus[:, :], in0=dr[:, :], scalar=2.0, in1=r,
                                                       op0=ALU.subtract, op1=ALU.mult).then_inc(newton, 1)
                        dve.wait_ge(newton, 2 * g + 2)
                        if g >= 2:
                            dve.wait_ge(out_done, g - 1)
                        nc.vector.scalar_tensor_tensor(out=on[:, g % 2, :], in0=OD[g % NOD][:, 0:W // 2], scalar=-1.0,
                                                       in1=minus[:, :], op0=ALU.mult, op1=ALU.mult).then_inc(on_ready, 1)
                for g in range(NG):
                    if PROJ[g] == u:
                        qt = GROUPS[g][0]
                        dve.wait_ge(out_done, g + 1)
                        if g:
                            dve.wait_ge(att_added, g)
                        nc.vector.tensor_tensor(yacc[:, qt, :], OD[g % NOD][:, 0:D], yacc[:, qt, :],
                                                ALU.add).then_inc(att_added, 1)
                for s in early(u - 1) + late(u - 1):
                    prepare_q(s)
                for s in early(u):
                    prepare(s)

        @block.tensor
        def _(pe):
            mm = nc.tensor.matmul
            pe.wait_ge(consts, 10)

            def transpose_x(c):
                pe.wait_ge(xn_ready, c + 1)
                if c >= 2:
                    pe.wait_ge(xnT_ready, c - 1)
                for t in range(CH):
                    last = nc.tensor.transpose(bank[c % 2][:, P * t:P * t + P], xn[:, CH * c + t, :], ident[:, :])
                last.then_inc(xT_done, 1)

            transpose_x(0)
            pe.wait_ge(wkv_in, 48)
            for c in range(NC):
                pe.wait_ge(xnT_ready, c + 1)
                for tile in range(CH * c, CH * c + CH):
                    if c:
                        pe.wait_ge(lg_ready, tile - CH + 1)
                    mm(bank[4 + tile % CH][:, 0:KV * HD + E], xnT[:, P * tile:P * tile + P], wvg_sb[:, :], start=True,
                       stop=True).then_inc(v_done, 1)
                if c + 1 < NC:
                    transpose_x(c + 1)
                for p in range(2):
                    if c:
                        pe.wait_ge(kl_ready, 2 * (c - 1) + p + 1)
                    mm(bank[2 + p][:, :], wk_sb[:, P * p:P * p + P], xnT[:, W * c:W * c + W], start=True,
                       stop=True).then_inc(k_done, 1)

            def prepare(step):
                kind, g, h, c = step
                if PREP[step] >= NM:
                    before = STREAM[PREP[step] - NM]
                    if before[0] == "M":
                        pe.wait_ge(pre_used, MORDER[before] + 1)
                    if before[0] == "Q":
                        pe.wait_ge(ql_ready, 2 * (before[1] + 1))
                    if before[0] == "R":
                        pe.wait_ge(row_ready, before[1] + 1)
                    if before[0] == "C":
                        pe.wait_ge(combT_ready, before[1] + 1)
                if kind == "C":
                    if g == 0:
                        pe.wait_ge(comb_ready, 1)
                    for t in range(CH):
                        last = nc.tensor.transpose(ring(step)[0:NE, P * t:P * t + P], comb[:, CH * g + t, :], ident[:, :])
                    last.then_inc(cT_done, 1)
                if kind == "Q":
                    qt, kv = GROUPS[g]
                    if g == 0:
                        pe.wait_ge(wq_in, 16)
                    for a in range(2):
                        pair = 2 * kv + a
                        last = mm(ring(step)[:, P * a:P * a + P], wq_sb[:, P * pair:P * pair + P],
                                  xnT[:, P * qt:P * qt + P], start=True, stop=True)
                    last.then_inc(q_done, 1)
                if kind == "M":
                    at, w = max_chunks(g)[c]
                    if h == 0 and c == 0:
                        pe.wait_ge(qh_ready, 2 * (g + 1))
                        pe.wait_ge(kdup, 2 * NC + 1)
                    mm(ring(step)[:, 0:w], q_hh[0:HD, g % NQ, P * h:P * h + P],
                       k_h1[0:HD, GROUPS[g][1], at:at + w], start=True, stop=True).then_inc(pre_done, 1)
                if kind == "R":
                    pe.wait_ge(diag_ready, g + 1)
                    mm(ring(step)[0:HD + 1, :], ones_r[:, :], diag[:, g % 2, :], start=True, stop=True).then_inc(row_done, 1)

            pe.wait_ge(lg_ready, NT)
            pe.wait_ge(w1_in, 48)
            pe.wait_ge(w2_in, 64)
            for n in range(NF + 1):
                if n < NF:
                    c, e = n // NE, n % NE
                    if n == 4:
                        pe.wait_ge(kl_ready, 2 * NC)
                    if n >= 3:
                        pe.wait_ge(h_ready, n - 2)
                    mm(hidden(n)[:, :], w1_sb[:, e, :], xnT[:, W * c:W * c + W], start=True,
                       stop=True).then_inc(h_done, 1)
                if n:
                    m = n - 1
                    c, e = m // NE, m % NE
                    pe.wait_ge(h_ready, m + 1)
                    if m >= 2:
                        pe.wait_ge(y_added, m - 1)
                    if e == E:
                        pe.wait_ge(combT_ready, c + 1)
                    for t in range(CH):
                        dst = YB[m % 2][:, P * t:P * t + P]
                        last = mm(dst, hT[:, m % 3, P * t:P * t + P], w2_sb[:, e, :], start=True, stop=e < E)
                        if e == E:
                            last = mm(dst, combT[:, P * (CH * c + t):P * (CH * c + t) + P], b2_sb[:, :], start=False,
                                      stop=True)
                    last.then_inc(y_done, 1)
                for s in EARLY.get(n, []):
                    prepare(s)

            pe.wait_ge(h_ready, NF)
            pe.wait_ge(wo_in, 16)
            for u in range(END):
                if u < NU:
                    g, i, j = UNITS[u]
                    kv = GROUPS[g][1]
                    if i == 0:
                        pe.wait_ge(q_twice, g + 1)
                        pe.wait_ge(ql_ready, 2 * (g + 1))
                        pe.wait_ge(row_ready, g + 1)
                    if u >= NST:
                        pe.wait_ge(exp_ready, u - NST + 1)
                    dst, keys = ST[u % NST][:, :], slice(P * j, P * j + P)
                    mm(dst, k_hl[:, kv, keys], q_hh[:, g % NQ, :], start=True, stop=False)
                    mm(dst, k_h1[:, kv, keys], q_lm[:, g % NQ, :], start=False, stop=True).then_inc(st_done, 1)
                for s in early(u):
                    prepare(s)
                for g in range(NG):
                    if PROJ[g] == u:
                        pe.wait_ge(on_ready, g + 1)
                        for a in range(2):
                            last = mm(OD[g % NOD][:, 0:D], on[:, g % 2, P * a:P * a + P],
                                      wo_sb[:, 2 * GROUPS[g][1] + a, :], start=a == 0, stop=a == 1)
                        last.then_inc(out_done, 1)
                for v in range(max(u - BATCH - 1, 0), min(u, NU)):
                    if PV[v] != u:
                        continue
                    g, i, j = UNITS[v]
                    kv = GROUPS[g][1]
                    if i == 0:
                        pe.wait_ge(masked, g + 1)
                        if g == 1:
                            pe.wait_ge(y_added, NF)
                        if g >= NOD:
                            pe.wait_ge(att_added, g - NOD + 1)
                    pe.wait_ge(exp_ready, v + 1)
                    for r in range(2):
                        last = mm(OD[g % NOD][HD * r:HD * r + HD, 0:W // 2], v_sb[:, j, HD * kv:HD * kv + HD],
                                  pT[:, v % NP, W // 2 * r:W // 2 * (r + 1)], start=i == 0, stop=i == COUNT[g] - 1)
                    last.then_inc(pv_done, 1)
                for g in range(NG):
                    if DEN[g] == u:
                        pe.wait_ge(summed, ADDS[LAST[g]])
                        for r in range(2):
                            last = mm(OD[g % NOD][HD * r:HD * r + HD, W // 2:W], ones[:, 0:HD],
                                      acc[:, g % 2, W // 2 * r:W // 2 * (r + 1)], start=True, stop=True)
                        last.then_inc(den_done, 1)
                for s in late(u):
                    prepare(s)


def kernel(L0_attn_hidden_states, L0_attn_Wq, L0_attn_Wk, L0_attn_Wv, L0_attn_Wo, L0_ffn_gate_w, L0_ffn_gate_b,
           L0_ffn_sw1, L0_ffn_sb1, L0_ffn_sw2, L0_ffn_sb2, L0_ffn_w1, L0_ffn_b1, L0_ffn_w2, L0_ffn_b2):
    import numpy as np
    import concourse.bacc as bacc
    from concourse import mybir as mb
    from concourse.bass_utils import run_bass_kernel_spmd

    def a(v):
        return np.asarray(v)

    wo = a(L0_attn_Wo).T.reshape(KV, 2, 2, HD, D).transpose(1, 3, 0, 2, 4).reshape(P, H // 2, D)
    laid = {
        "x": a(L0_attn_hidden_states).reshape(S, D), "wqT": a(L0_attn_Wq).T, "wkT": a(L0_attn_Wk).T,
        "wvT": a(L0_attn_Wv).T, "woT": wo, "gw": a(L0_ffn_gate_w), "gb": np.broadcast_to(a(L0_ffn_gate_b), (P, E)),
        "b1T": np.concatenate([a(L0_ffn_b1), a(L0_ffn_sb1)[None]]).T, "w1": a(L0_ffn_w1), "sw1": a(L0_ffn_sw1),
        "w2": a(L0_ffn_w2), "sw2": a(L0_ffn_sw2), "b2": a(L0_ffn_b2), "sb2": a(L0_ffn_sb2).reshape(1, D),
    }
    nc = bacc.Bacc("TRN2", target_bir_lowering=False, num_devices=1)
    arrays, args = {}, []
    for name, v in laid.items():
        v = np.ascontiguousarray(v)
        arrays[f"in_{name}"] = v
        args.append(nc.dram_tensor(f"in_{name}", v.shape, mb.dt.from_np(v.dtype), kind="ExternalInput").ap())
    out = nc.dram_tensor("out", (S, D), mb.dt.float32, kind="ExternalOutput").ap()
    layer(nc, *args, out)
    r = run_bass_kernel_spmd(nc, [arrays], core_ids=[0])
    return r.results[0]["out"].reshape(1, S, D)
```
